# Optimizing a Trainium2 kernel written in Bass

```python
import numpy as np
import jax
import jax.numpy as jnp

def _softmax(x, axis=-1):
    return jax.nn.softmax(x, axis=axis)

def _gelu(x):
    return jax.nn.gelu(x, approximate=True)

def _silu(x):
    return jax.nn.silu(x)

def _sigmoid(x):
    return jax.nn.sigmoid(x)

def _layernorm(x, axis=-1, eps=1e-05):
    m = jnp.mean(x, axis=axis, keepdims=True)
    v = jnp.var(x, axis=axis, keepdims=True)
    return (x - m) / jnp.sqrt(v + eps)

def _scatter_add(tgt, idx, src, axis=0):
    return tgt.at[idx].add(src)

def _segment_sum(src, seg, n):
    return jax.ops.segment_sum(src, seg, n)
kernel_name = 'mk_decoder_preln_d1_seqx_r8_658dee'

def setup_inputs(seed: int=0):
    np.random.seed(seed)
    _w = jnp.asarray

    def _rec_inputs():
        import jax
        import jax.numpy as jnp
        _rk = jax.random.key(seed)
        x = -0.000125 + 0.9999 * jax.random.normal(jax.random.fold_in(_rk, 1), (2, 512, 128), jnp.float32)
        _lenS = 512 - jax.random.randint(jax.random.fold_in(_rk, 7), (2,), 0, max(1, 512 // 4) + 1, jnp.int32)
        _lenS2 = 32 - jax.random.randint(jax.random.fold_in(_rk, 8), (2,), 0, max(1, 32 // 4) + 1, jnp.int32)
        _ctx_768P = jax.random.normal(jax.random.fold_in(_rk, 11), (2, 16, 96), jnp.float32)
        _ctx_768c = jax.random.dirichlet(jax.random.fold_in(_rk, 511), 0.3 * jnp.ones((16,), jnp.float32), (2, 32))
        _ctx_768t = jnp.einsum('bsk,bkd->bsd', _ctx_768c, _ctx_768P)
        _ctx_768t = _ctx_768t * jax.lax.rsqrt(jnp.mean(jnp.square(_ctx_768t)) + 1e-12) * 0.953939
        ctx_768 = 0.00272024 + 0.999456 * (_ctx_768t + 0.3 * jax.random.normal(jax.random.fold_in(_rk, 611), (2, 32, 96), jnp.float32))
        return (x, ctx_768)
    x, ctx_768 = _rec_inputs()

    def _L0_attn_setup():
        import jax, jax.numpy as jnp
        import numpy as np
        N_HEAD = 16
        NEG_BIG = 10000000000.0
        key = jax.random.key(seed)
        k1, k2, k3 = jax.random.split(key, 3)
        B, T, D = (2, 256, 128)
        x = jax.random.normal(k1, (B, T, D), dtype=jnp.float32)
        W_attn = jax.random.normal(k2, (D, 3 * D), dtype=jnp.float32) * 0.02
        b_attn = jnp.zeros((3 * D,), dtype=jnp.float32)
        W_proj = jax.random.normal(k3, (D, D), dtype=jnp.float32) * 0.02
        b_proj = jnp.zeros((D,), dtype=jnp.float32)
        return {'x': x, 'W_attn': W_attn, 'b_attn': b_attn, 'W_proj': W_proj, 'b_proj': b_proj}
    _L0_attn_all = _L0_attn_setup()
    _L0_attn_in = {k: v for k, v in _L0_attn_all.items() if k in ('W_attn', 'b_attn', 'W_proj', 'b_proj')}
    del _L0_attn_all

    def _L0_xattn_setup():
        import jax, jax.numpy as jnp
        import numpy as np
        B, N, M = (8, 512, 77)
        Q_DIM, CTX_DIM = (128, 96)
        H, D = (16, 64)
        INNER = H * D
        key = jax.random.key(seed)
        ks = jax.random.split(key, 7)
        x = jax.random.normal(ks[0], (B, N, Q_DIM), dtype=jnp.float32)
        context = jax.random.normal(ks[1], (B, M, CTX_DIM), dtype=jnp.float32)
        Wq = jax.random.normal(ks[2], (Q_DIM, INNER), dtype=jnp.float32) * Q_DIM ** (-0.5)
        Wk = jax.random.normal(ks[3], (CTX_DIM, INNER), dtype=jnp.float32) * CTX_DIM ** (-0.5)
        Wv = jax.random.normal(ks[4], (CTX_DIM, INNER), dtype=jnp.float32) * CTX_DIM ** (-0.5)
        Wo = jax.random.normal(ks[5], (INNER, Q_DIM), dtype=jnp.float32) * INNER ** (-0.5)
        bo = jax.random.normal(ks[6], (Q_DIM,), dtype=jnp.float32) * 0.01
        return {'x': x, 'context': context, 'Wq': Wq, 'Wk': Wk, 'Wv': Wv, 'Wo': Wo, 'bo': bo}
    _L0_xattn_all = _L0_xattn_setup()
    _L0_xattn_in = {k: v for k, v in _L0_xattn_all.items() if k in ('Wq', 'Wk', 'Wv', 'Wo', 'bo')}
    del _L0_xattn_all

    def _L0_ffn_setup():
        import jax, jax.numpy as jnp
        import numpy as np
        S, B, H, I, E = (64, 2, 128, 352, 8)
        key = jax.random.key(seed)
        ks = jax.random.split(key, 5)
        return {'hidden_states': jax.random.normal(ks[0], (S, B, H), dtype=jnp.float32), 'router_w': jax.random.normal(ks[1], (E, H), dtype=jnp.float32) * 0.02, 'gate_w': jax.random.normal(ks[2], (E, I, H), dtype=jnp.float32) * 0.02, 'up_w': jax.random.normal(ks[3], (E, I, H), dtype=jnp.float32) * 0.02, 'down_w': jax.random.normal(ks[4], (E, H, I), dtype=jnp.float32) * 0.02}
    _L0_ffn_all = _L0_ffn_setup()
    _L0_ffn_in = {k: v for k, v in _L0_ffn_all.items() if k in ('router_w', 'gate_w', 'up_w', 'down_w')}
    del _L0_ffn_all
    return {'x': x, 'ctx_768': ctx_768, 'L0_attn_W_attn': _L0_attn_in['W_attn'], 'L0_attn_b_attn': _L0_attn_in['b_attn'], 'L0_attn_W_proj': _L0_attn_in['W_proj'], 'L0_attn_b_proj': _L0_attn_in['b_proj'], 'L0_xattn_Wq': _L0_xattn_in['Wq'], 'L0_xattn_Wk': _L0_xattn_in['Wk'], 'L0_xattn_Wv': _L0_xattn_in['Wv'], 'L0_xattn_Wo': _L0_xattn_in['Wo'], 'L0_xattn_bo': _L0_xattn_in['bo'], 'L0_ffn_router_w': _L0_ffn_in['router_w'], 'L0_ffn_gate_w': _L0_ffn_in['gate_w'], 'L0_ffn_up_w': _L0_ffn_in['up_w'], 'L0_ffn_down_w': _L0_ffn_in['down_w']}

def reference(x, ctx_768, L0_attn_W_attn, L0_attn_b_attn, L0_attn_W_proj, L0_attn_b_proj, L0_xattn_Wq, L0_xattn_Wk, L0_xattn_Wv, L0_xattn_Wo, L0_xattn_bo, L0_ffn_router_w, L0_ffn_gate_w, L0_ffn_up_w, L0_ffn_down_w):
    import jax
    import jax.numpy as jnp

    def _L0_attn_ref(x, W_attn, b_attn, W_proj, b_proj):
        import jax, jax.numpy as jnp
        import numpy as np
        N_HEAD = 16
        NEG_BIG = 10000000000.0
        B, T, D = x.shape
        H = N_HEAD
        dh = D // H
        qkv = x @ W_attn + b_attn
        q, k, v = jnp.split(qkv, 3, axis=-1)
        q = q.reshape(B, T, H, dh).transpose(0, 2, 1, 3)
        k = k.reshape(B, T, H, dh).transpose(0, 2, 1, 3)
        v = v.reshape(B, T, H, dh).transpose(0, 2, 1, 3)
        w = jnp.einsum('bhqd,bhkd->bhqk', q, k)
        w = w / jnp.sqrt(jnp.float32(dh))
        bias = jnp.tril(jnp.ones((T, T), dtype=w.dtype))
        w = w * bias - NEG_BIG * (1.0 - bias)
        w = jax.nn.softmax(w, axis=-1)
        a = jnp.einsum('bhqk,bhkd->bhqd', w, v)
        a = a.transpose(0, 2, 1, 3).reshape(B, T, D)
        return a @ W_proj + b_proj

    def _L0_xattn_ref(x, context, Wq, Wk, Wv, Wo, bo):
        import jax, jax.numpy as jnp
        import numpy as np
        B, N, M = (8, 512, 77)
        Q_DIM, CTX_DIM = (128, 96)
        H, D = (16, 64)
        INNER = H * D
        scale = D ** (-0.5)

        def heads(t):
            b, s, _ = t.shape
            return t.reshape(b, s, H, D).transpose(0, 2, 1, 3)
        q = heads(x @ Wq)
        k = heads(context @ Wk)
        v = heads(context @ Wv)
        scores = jnp.einsum('bhid,bhjd->bhij', q, k) * scale
        attn = jax.nn.softmax(scores, axis=-1)
        out = jnp.einsum('bhij,bhjd->bhid', attn, v)
        out = out.transpose(0, 2, 1, 3).reshape(x.shape[0], x.shape[1], INNER)
        return out @ Wo + bo

    def _L0_ffn_ref(hidden_states, router_w, gate_w, up_w, down_w):
        import jax, jax.numpy as jnp
        import numpy as np
        S, B, H, I, E = (64, 2, 128, 352, 8)
        router_logits = jnp.einsum('sbh,eh->sbe', hidden_states, router_w)
        routing_indices = jnp.argmax(router_logits, axis=-1)
        out = jnp.zeros_like(hidden_states)
        for e in range(E):
            mask = (routing_indices == e)[..., None]
            xe = jnp.where(mask, hidden_states, 0.0)
            g = jnp.einsum('sbh,ih->sbi', xe, gate_w[e])
            u = jnp.einsum('sbh,ih->sbi', xe, up_w[e])
            ye = jnp.einsum('sbi,hi->sbh', jax.nn.silu(g) * u, down_w[e])
            out = out + jnp.where(mask, ye, 0.0)
        return out
    x = x + _L0_attn_ref(_layernorm(x, axis=-1), L0_attn_W_attn, L0_attn_b_attn, L0_attn_W_proj, L0_attn_b_proj)
    x = x + _L0_xattn_ref(_layernorm(x, axis=-1), ctx_768, L0_xattn_Wq, L0_xattn_Wk, L0_xattn_Wv, L0_xattn_Wo, L0_xattn_bo)
    x = x + _L0_ffn_ref(_layernorm(x, axis=-1), L0_ffn_router_w, L0_ffn_gate_w, L0_ffn_up_w, L0_ffn_down_w)
    return x

_drawn_inputs = setup_inputs


def setup_inputs(seed=0):
    import zlib

    import numpy as np

    out = dict(_drawn_inputs(seed))
    spreads = {'L0_attn_b_attn': (0.0, 0.425), 'L0_attn_b_proj': (0.0, 0.1)}
    factors = {'L0_attn_W_attn': 8.0,
     'L0_attn_W_proj': 3.21,
     'L0_xattn_bo': 6.196,
     'L0_ffn_router_w': 7.184,
     'L0_ffn_gate_w': 6.902,
     'L0_ffn_up_w': 6.842,
     'L0_ffn_down_w': 6.835}
    for name, (base, spread) in spreads.items():
        noise = np.random.default_rng([zlib.crc32(name.encode()), seed]).standard_normal(out[name].shape)
        drawn = base * np.exp(spread * noise) if base else spread * noise
        out[name] = jnp.asarray(drawn.astype(out[name].dtype))
    for name, factor in factors.items():
        out[name] = (out[name] * factor).astype(out[name].dtype)
    return out
```

```python
from contextlib import ExitStack

import concourse.bass as bass
from concourse import mybir

F32 = mybir.dt.float32
BF16 = mybir.dt.bfloat16
I32 = mybir.dt.int32
ALU = mybir.AluOpType
ACT = mybir.ActivationFunctionType
AX = mybir.AxisListType

P = 128
B, T, D = 2, 512, 128
QT = T // P
NT = B * QT
H, DH = 16, 8
GH = 4
NG = B * H // GH
GPB = H // GH
SC = 9 * DH
SA = SC + 3
VW = 32
CT, CW = 32, 96
XH, XD = 16, 64
XC = XH * XD // P
XS = XH * CT
E, I = 8, 352
IC = 3
IR = I - 2 * P
NS = (NT * P + E * (P - 1)) // P
EPS = 1e-5
UNITS = 12
KU = 2 * QT
CONST_W = 3 * P + E * NT + NS * E + E

SPLIT = {"q": 0, "k": 1}


def max_units():
    units = []
    for qt in reversed(range(QT)):
        heads = {3: 1, 2: 1, 1: 2, 0: 2}[qt]
        units += [(qt, j, heads) for j in range(0, GH, heads)]
    return units


def decoder_layer(nc, x, ctx_t, w_attn, b_attn_qk, b_attn_v, w_proj, b_proj, wq_t, wk, wv, wo, bo,
                  router_t, gate_up, down, consts, out):
    units = max_units()
    assert len(units) == UNITS

    with ExitStack() as ctx:
        def sb(name, shape, dt=F32):
            return ctx.enter_context(nc.sbuf_tensor(name, shape, dt))

        def sem(name):
            return ctx.enter_context(nc.semaphore(name))

        parts_dram = nc.dram_tensor("parts_dram", (B, 2, 3, P, T), BF16, kind="Internal").ap()
        routed_dram = nc.dram_tensor("routed_dram", (NS * P, D), F32, kind="Internal").ap()
        expert_out_dram = nc.dram_tensor("expert_out_dram", (NS * P, D), F32, kind="Internal").ap()

        cst = sb("cst", [P, CONST_W])
        ident = cst[:, 0:P]
        o0 = 3 * P
        tile_edges = cst[:, o0:o0 + E * NT].rearrange("p (e k) -> p e k", e=E)
        o0 += E * NT
        tile_index = cst[:, o0:o0 + NS * E].rearrange("p (s e) -> p s e", s=NS)
        first_rank = cst[:, o0 + NS * E:o0 + NS * E + E]
        cbf = sb("cbf", [P, 3 * P], BF16)
        ident_bf, causal_bf, before_bf = cbf[:, 0:P], cbf[:, P:2 * P], cbf[:, 2 * P:3 * P]
        ones_bf = sb("ones_bf", [P, P], BF16)
        ones_row = sb("ones_row", [3, T], BF16)
        neg_half = sb("neg_half", [P, NT])
        w_attn_sb = sb("w_attn_sb", [P, 3 * D])
        b_qk_sb = sb("b_qk_sb", [P, 2])
        b_v_sb = sb("b_v_sb", [P, D])
        w_proj_sb = sb("w_proj_sb", [P, D])
        b_proj_sb = sb("b_proj_sb", [P, D])
        bo_sb = sb("bo_sb", [P, D])
        ctx_sb = sb("ctx_sb", [CW, B * CT])
        router_sb = sb("router_sb", [P, E])

        x_sb = sb("x_sb", [P, NT, D])
        xb = sb("xb", [P, NT, D])
        xn = sb("xn", [P, NT, D])
        xn_t = sb("xn_t", [P, B, T])
        stat = sb("stat", [P, 3, NT, 6])
        mv = sb("mv", [P, 3, NT, 2])
        var_eps = sb("var_eps", [P, 3, NT])
        rstd = sb("rstd", [P, 3, NT])
        part = sb("part", [P, 2, 3, B, T], BF16)
        qs = sb("qs", [P, B * H, T], BF16)
        ks = sb("ks", [P, B * H, T], BF16)
        gate_up_sb = qs[:].rearrange("p h t -> p (h t)").bitcast(F32)[:, 0:E * 2 * I]
        down_sb = ks[:].rearrange("p h t -> p (h t)").bitcast(F32)[:, 0:E * IC * D]
        v_sb = sb("v_sb", [P, NT, H, DH])
        vg = sb("vg", [P, QT, GH, VW])
        mx = sb("mx", [P, QT, GH])
        mrest = sb("mrest", [P, QT, GH])
        mparts = sb("mparts", [P, QT, 3, GH], BF16)
        m_t = sb("m_t", [3 * GH, T], BF16)
        probs = sb("probs", [P, QT, GH, T])
        room = probs[:].rearrange("p a h t -> p (a h t)")
        full = room[:, 0:2 * B * T].rearrange("p (w b t) -> p w b t", w=2, b=B)
        rest = room[:, 2 * B * T:4 * B * T].rearrange("p (w b t) -> p w b t", w=2, b=B)
        o0, n = 4 * B * T, XH * XD
        wk_sb = room[0:CW, o0:o0 + n]
        wv_sb = room[0:CW, o0 + n:o0 + 2 * n]
        wq_sb = room[:, o0 + 2 * n:o0 + 3 * n].rearrange("p (c d) -> p c d", c=XC)
        wo_sb = room[:, o0 + 3 * n:o0 + 4 * n].rearrange("p (c d) -> p c d", c=XC)
        routed = room[:, 0:NS * D].rearrange("p (n d) -> p n d", n=NS)
        y_back = room[:, NS * D:(NS + NT) * D].rearrange("p (n d) -> p n d", n=NT)
        res = room[:, (NS + NT) * D:(NS + 2 * NT) * D].rearrange("p (n d) -> p n d", n=NT)
        o_sb = sb("o_sb", [P, T])
        attn = sb("attn", [P, NT, H, DH])
        den = sb("den", [P, QT, GH])
        k_blk = sb("k_blk", [P, XC, B, 2, CT])
        v_blk = sb("v_blk", [P, XC, B, 2, CT])
        a_sb = sb("a_sb", [P, B, XS])
        bm_sb = sb("bm_sb", [P, B, 4, D])
        tr_sb = sb("tr_sb", [P, 4, P])
        x1 = sb("x1", [P, NT, D])
        x1b = sb("x1b", [P, NT, D])
        xn2 = sb("xn2", [P, 2, D])
        xm = sb("xm", [P, 2, XH])
        xe = sb("xe", [P, 2, XS])
        xp = sb("xp", [P, 2, XS])
        xs_sum = sb("xs_sum", [P, 2, XH])
        xp_t = sb("xp_t", [P, 2, XS])
        x2 = sb("x2", [P, NT, D])
        xn3 = sb("xn3", [P, NT, D])
        logit_max = sb("logit_max", [P, NT])
        first = sb("first", [P, NT, E])
        first_max = sb("first_max", [P, NT])
        chosen = sb("chosen", [P, NT, E])
        chosen_bf = sb("chosen_bf", [P, NT, E], BF16)
        over = sb("over", [P, E, NT])
        expert_tiles = sb("expert_tiles", [P, E])
        zeros_e = sb("zeros_e", [P, E])
        tiles_end = sb("tiles_end", [P, E])
        run_start = sb("run_start", [P, E])
        slot_e = sb("slot_e", [P, NT, E])
        slot_f = sb("slot_f", [P, NT])
        slot = sb("slot", [P, NT], I32)
        past = sb("past", [P, NS, E])
        tile_expert_f = sb("tile_expert_f", [P, 2, NS])
        tile_expert = sb("tile_expert", [P, 2, NS], I32)
        zeros_x = sb("zeros_x", [P, D])
        routed_t = sb("routed_t", [P, 2, P])
        act_gate = sb("act_gate", [P, 2, I])
        hidden = sb("hidden", [P, 2, I])
        hidden_t = sb("hidden_t", [P, 2, IC, P])
        y_sb = sb("y_sb", [P, 2, D])

        ps = ctx.enter_context(nc.psum_tensor("ps", [P, 8, T], F32))

        names = """x0_in x1_in w_attn_in bias_in const_in ctx_in wkv_in wqo_in proj_in xbias_in router_in experts_in
            const_ready ones_ready dve_chain act_chain pool_chain pe_chain
            ln1_stats rstd1 xn_ready xn_tr xn_t_ready qk_mm qk_read v_mm v_ready
            full_ready hi_ready rest_ready mid_ready low_ready parts_out0 parts_out1 stack0_in stack1_in ones_in
            kt_mm kt_read vt_mm vt_read kv_blk_zero a_mm a_read bm_mm bm_read
            unit_ready unit_read mparts_ready m_tr m_t_ready m_rows_even m_rows_odd
            st_ready exp_done masked v_copied pv_done o_copied o_tr attn_ready
            attn_tr attn_t_ready x1_mm x1_ready x1b_ready ln2_stats rstd2 xn2_ready xn2_tr xn2_t_ready
            xs_mm xs_taken xsub_ready xexp_done xinv_ready xp_ready xp_tr xp_t_ready x2_mm x2_ready
            ln3_stats rstd3 xn3_ready xn3_tr xn3_t_ready logits_mm chosen_ready counts_mm counts_read slot_ready
            experts_known zero_ready zero_out scattered routed_in routed_tr routed_t_ready
            gate_mm up_mm silu_done hidden_ready hidden_tr hidden_t_ready y_mm y_ready y_out0 y_out1 gathered
            res_ready out_done vg_ready xb_ready""".split()
        s = {n: sem(n) for n in names}

        block = ctx.enter_context(nc.Block())

        def bank(n):
            return ps[:, n, :]

        S_BANK = (0, 1)
        ST_BANK = (2, 4)
        O_BANK = 6
        MISC = 7

        @block.sync
        def _(sp):
            sp.dma_start(x_sb[:, 0:QT, :], x[0].rearrange("(t p) d -> p t d", p=P)).then_inc(s["x0_in"], 16)
            sp.dma_start(cst[:], consts).then_inc(s["const_in"], 16)
            sp.dma_start(w_attn_sb[:], w_attn).then_inc(s["w_attn_in"], 16)
            sp.dma_start(x_sb[:, QT:NT, :], x[1].rearrange("(t p) d -> p t d", p=P)).then_inc(s["x1_in"], 16)
            sp.dma_start(ctx_sb[:], ctx_t).then_inc(s["ctx_in"], 16)
            sp.dma_start(wk_sb, wk).then_inc(s["wkv_in"], 16)
            sp.dma_start(wv_sb, wv).then_inc(s["wkv_in"], 16)
            sp.dma_start(wq_sb, wq_t.rearrange("(c p) d -> p c d", p=P)).then_inc(s["wqo_in"], 16)
            sp.dma_start(wo_sb, wo.rearrange("(c p) d -> p c d", p=P)).then_inc(s["wqo_in"], 16)
            for b in range(B):
                out_sem, in_sem = s[f"parts_out{b}"], s[f"stack{b}_in"]
                sp.wait_ge(s["hi_ready"], 2 * b + 2)
                sp.dma_start(parts_dram[b, :, 0].rearrange("s p t -> p s t"), part[:, :, 0, b, :]).then_inc(out_sem, 16)
                sp.wait_ge(s["mid_ready"], 2 * b + 2)
                sp.dma_start(parts_dram[b, :, 1].rearrange("s p t -> p s t"), part[:, :, 1, b, :]).then_inc(out_sem, 16)
                sp.wait_ge(s["low_ready"], 2 * b + 2)
                sp.dma_start(parts_dram[b, :, 2].rearrange("s p t -> p s t"), part[:, :, 2, b, :]).then_inc(out_sem, 16)
                sp.wait_ge(out_sem, 48)
                for j in range(9):
                    rows = slice(j * DH, (j + 1) * DH)
                    hs = slice(b * H, (b + 1) * H)
                    sp.dma_start(qs[rows, hs, :],
                                 parts_dram[b, 0, j // 3].rearrange("(h d) t -> d h t", d=DH)).then_inc(in_sem, 16)
                    sp.dma_start(ks[rows, hs, :],
                                 parts_dram[b, 1, j % 3].rearrange("(h d) t -> d h t", d=DH)).then_inc(in_sem, 16)
            for i in range(NG):
                sp.wait_ge(s["m_t_ready"], i + 1)
                for c in range(3):
                    sp.dma_start(qs[SC + c:SC + c + 1, GH * i:GH * (i + 1), :],
                                 m_t[GH * c:GH * (c + 1), :]).then_inc(s["m_rows_odd" if i % 2 else "m_rows_even"], 16)
            sp.wait_ge(s["st_ready"], KU * NG)
            sp.dma_start(gate_up_sb, gate_up).then_inc(s["experts_in"], 16)
            sp.dma_start(down_sb, down).then_inc(s["experts_in"], 16)
            sp.wait_ge(s["scattered"], 16 * NT)
            for n in range(3):
                k = NS // 3
                sp.dma_start(routed[:, n * k:(n + 1) * k, :],
                             routed_dram[n * k * P:(n + 1) * k * P].rearrange("(s p) d -> p s d", p=P))\
                    .then_inc(s["routed_in"], 16)
            for n in range(NS):
                sp.wait_ge(s["y_ready"], n + 1)
                sp.dma_start(expert_out_dram[n * P:(n + 1) * P], y_sb[:, n % 2, :]).then_inc(s[f"y_out{n % 2}"], 16)
            for n in range(NT):
                sp.wait_ge(s["res_ready"], n + 1)
                sp.dma_start(out[n // QT, (n % QT) * P:(n % QT + 1) * P, :], res[:, n, :]).then_inc(s["out_done"], 16)
            sp.wait_ge(s["out_done"], 16 * NT)

        @block.scalar
        def _(act):
            def copy(dst, src):
                return nc.scalar.activation(dst, src, ACT.Copy)

            act.dma_start(b_qk_sb[:], b_attn_qk).then_inc(s["bias_in"], 16)
            act.dma_start(b_v_sb[:], b_attn_v.partition_broadcast(P)).then_inc(s["bias_in"], 16)
            act.dma_start(w_proj_sb[:], w_proj).then_inc(s["proj_in"], 16)
            act.dma_start(b_proj_sb[:], b_proj.partition_broadcast(P)).then_inc(s["xbias_in"], 16)
            act.dma_start(bo_sb[:], bo.partition_broadcast(P)).then_inc(s["xbias_in"], 16)
            act.dma_start(router_sb[:], router_t).then_inc(s["router_in"], 16)
            act.wait_ge(s["ones_ready"], 1)
            act.dma_start(ks[SC:SA, :, :], ones_row[:, :].unsqueeze(1).to_broadcast([3, B * H, T]))\
                .then_inc(s["ones_in"], 16)
            act.wait_ge(s["zero_ready"], 1)
            act.dma_start(routed_dram.rearrange("(s p) d -> p s d", p=P),
                          zeros_x[:, :].unsqueeze(1).to_broadcast([P, NS, D])).then_inc(s["zero_out"], 16)
            for b in range(B):
                act.wait_ge(s["xn_tr"], b + 1)
                copy(xn_t[:, b, :], bank(b)).then_inc(s["xn_t_ready"], 1)
            act.wait_ge(s["bias_in"], 32)
            for b in range(B):
                for w in range(2):
                    n = 2 * b + w
                    act.wait_ge(s["qk_mm"], n + 1)
                    nc.scalar.activation(full[:, w, b, :], bank(2 + w), ACT.Identity,
                                         bias=b_qk_sb[:, w:w + 1]).then_inc(s["full_ready"], 1)
                    nc.scalar.activation(part[:, w, 0, b, :], bank(2 + w), ACT.Identity,
                                         bias=b_qk_sb[:, w:w + 1]).then_inc(s["hi_ready"], 1)
                for w in range(2):
                    act.wait_ge(s["rest_ready"], 2 * b + w + 1)
                    copy(part[:, w, 1, b, :], rest[:, w, b, :]).then_inc(s["mid_ready"], 1)
            act.wait_ge(s["kv_blk_zero"], 2)
            for w, (mm, read, blk) in enumerate((("kt_mm", "kt_read", k_blk), ("vt_mm", "vt_read", v_blk))):
                act.wait_ge(s[mm], 1)
                for half in range(2):
                    rows = slice(64 * half, 64 * half + 64)
                    last = copy(blk[rows, :, :, half, :],
                                ps[rows, 4 + w, :].rearrange("p (c b j) -> p c b j", c=XC, b=B))
                    last.then_inc(s[read], 1)
            for n in range(2):
                act.wait_ge(s["a_mm"], n + 1)
                copy(a_sb[:, :, n * 256:(n + 1) * 256].rearrange("p b (c j) -> p b c j", c=4),
                     ps[:, 6 + n, :].rearrange("p (c b j) -> p b c j", c=4, b=B)).then_inc(s["a_read"], 1)
            act.wait_ge(s["bm_mm"], 1)
            copy(bm_sb[:].rearrange("p b c d -> p (b c d)"),
                 ps[:, 4:6, :].rearrange("p a n -> p (a n)")).then_inc(s["bm_read"], 1)

            def o_copy(i):
                act.wait_ge(s["pv_done"], QT * (i + 1))
                if i >= 1:
                    act.wait_ge(s["o_tr"], i)
                copy(o_sb[:, :], bank(O_BANK)).then_inc(s["o_copied"], 1)

            def m_copy(i):
                act.wait_ge(s["m_tr"], i + 1)
                if i >= 1:
                    act.wait_ge(s["m_rows_even" if i % 2 else "m_rows_odd"], 48 * ((i - 1) // 2 + 1))
                copy(m_t[:, :], bank(MISC)[0:3 * GH, 0:T // 2].bitcast(BF16)).then_inc(s["m_t_ready"], 1)

            def exps(i, kt):
                for pair in range(2):
                    u = KU * i + 2 * kt + pair
                    act.wait_ge(s["st_ready"], u + 1)
                    if i >= 1:
                        act.wait_ge(s["pv_done"], QT * (i - 1) + kt + 1)
                    bk = ST_BANK[pair]
                    nc.scalar.activation(probs[:, kt, 2 * pair:2 * pair + 2, kt * P:T],
                                         ps[:, bk:bk + 2, kt * P:T], ACT.Exp,
                                         scale=float(DH) ** -0.5).then_inc(s["exp_done"], 1)

            m_copy(0)
            for i in range(NG + 1):
                if i < NG:
                    exps(i, 0)
                if i >= 1:
                    o_copy(i - 1)
                if i + 1 < NG:
                    m_copy(i + 1)
                if i < NG:
                    for kt in range(1, QT):
                        exps(i, kt)

            def st_a(t):
                act.wait_ge(s["attn_tr"], t + 1)
                copy(tr_sb[:, 0, :], bank(0)[:, 0:P]).then_inc(s["attn_t_ready"], 1)

            def st_c(t):
                act.wait_ge(s["xn2_tr"], t + 1)
                copy(tr_sb[:, 1, :], bank(1)[:, 0:P]).then_inc(s["xn2_t_ready"], 1)

            def st_d(t):
                act.wait_ge(s["xsub_ready"], t + 1)
                nc.scalar.activation(xe[:, t % 2, :], xe[:, t % 2, :], ACT.Exp,
                                     scale=float(XD) ** -0.5).then_inc(s["xexp_done"], 1)

            def st_e(t):
                act.wait_ge(s["xp_tr"], t + 1)
                if t >= 2:
                    act.wait_ge(s["x2_mm"], t - 1)
                copy(xp_t[:, t % 2, :], bank(4)).then_inc(s["xp_t_ready"], 1)

            def st_f(t):
                act.wait_ge(s["xn3_tr"], t + 1)
                copy(tr_sb[:, 2, :], bank(1)[:, P:2 * P]).then_inc(s["xn3_t_ready"], 1)

            for step in range(NT + 3):
                for fn, lag in ((st_a, 0), (st_c, 0), (st_d, 1), (st_e, 2), (st_f, 3)):
                    if 0 <= step - lag < NT:
                        fn(step - lag)

            def mx_a(n):
                act.wait_ge(s["routed_tr"], n + 1)
                if n >= 2:
                    act.wait_ge(s["up_mm"], n - 1)
                copy(routed_t[:, n % 2, :], bank(0)[:, 0:P]).then_inc(s["routed_t_ready"], 1)

            def mx_b(n):
                act.wait_ge(s["gate_mm"], n + 1)
                if n >= 2:
                    act.wait_ge(s["hidden_ready"], n - 1)
                nc.scalar.activation(act_gate[:, n % 2, :], bank(1 + n % 2)[:, 0:I], ACT.Silu)\
                    .then_inc(s["silu_done"], 1)

            def mx_c(n):
                act.wait_ge(s["hidden_tr"], n + 1)
                if n >= 2:
                    act.wait_ge(s["y_mm"], n - 1)
                copy(hidden_t[:, n % 2, 0:2, :], bank(5)[:, 0:2 * P].rearrange("p (c q) -> p c q", c=2))
                copy(hidden_t[0:IR, n % 2, 2, :], bank(5)[0:IR, 2 * P:3 * P]).then_inc(s["hidden_t_ready"], 1)

            for step in range(NS + 2):
                for fn, lag in ((mx_a, 0), (mx_b, 1), (mx_c, 2)):
                    if 0 <= step - lag < NS:
                        fn(step - lag)

        @block.gpsimd
        def _(pool):
            nc.gpsimd.memset(ones_row[:], 1.0).then_inc(s["ones_ready"], 1)
            nc.gpsimd.memset(neg_half[:], -0.5).then_inc(s["pool_chain"], 1)
            nc.gpsimd.memset(zeros_x[:], 0.0).then_inc(s["zero_ready"], 1)
            pool.wait_ge(s["pool_chain"], 1)
            chain = [1]

            def link(ins):
                chain[0] += 1
                ins.then_inc(s["pool_chain"], 1)
                pool.wait_ge(s["pool_chain"], chain[0])

            def inv_std(ln, lo, hi, name):
                link(nc.gpsimd.tensor_scalar(var_eps[:, ln, lo:hi], mv[:, ln, lo:hi, 1], EPS, None, ALU.add))
                nc.gpsimd.tensor_tensor(rstd[:, ln, lo:hi], var_eps[:, ln, lo:hi], neg_half[:, lo:hi], ALU.pow)\
                    .then_inc(s[name], 1)

            for b in range(B):
                pool.wait_ge(s["ln1_stats"], QT * (b + 1))
                inv_std(0, b * QT, (b + 1) * QT, "rstd1")
            link(nc.gpsimd.memset(vg[:], 0.0))
            link(nc.gpsimd.memset(vg[:, :, :, DH:DH + 1], 1.0))
            nc.gpsimd.memset(k_blk[:], 0.0).then_inc(s["kv_blk_zero"], 1)
            nc.gpsimd.memset(v_blk[:], 0.0).then_inc(s["kv_blk_zero"], 1)
            pool.wait_ge(s["x0_in"], 16)
            pool.wait_ge(s["x1_in"], 16)
            pool.wait_ge(s["xbias_in"], 32)
            nc.gpsimd.tensor_tensor(xb[:], x_sb[:], b_proj_sb[:, :].unsqueeze(1).to_broadcast([P, NT, D]), ALU.add)\
                .then_inc(s["xb_ready"], 1)
            pool.wait_ge(s["v_ready"], B)
            for i in range(NG):
                for kt in range(QT):
                    if i >= 1:
                        pool.wait_ge(s["pv_done"], QT * (i - 1) + kt + 1)
                    nc.gpsimd.tensor_copy(vg[:, kt, :, 0:DH],
                                          v_sb[:, QT * (i // GPB) + kt, GH * (i % GPB):GH * (i % GPB) + GH, :])\
                        .then_inc(s["vg_ready"], 1)
                    for pair in range(2):
                        pool.wait_ge(s["exp_done"], KU * i + 2 * kt + pair + 1)
                        blk = probs[:, kt, 2 * pair:2 * pair + 2, kt * P:(kt + 1) * P]
                        nc.gpsimd.affine_select(out=blk, in_=blk, compare_op=ALU.is_ge, fill=0.0, base=0,
                                                pattern=[[0, 2], [1, P]], channel_multiplier=-1)\
                            .then_inc(s["masked"], 1)

            def st_b(t):
                pool.wait_ge(s["ln2_stats"], t + 1)
                inv_std(1, t, t + 1, "rstd2")
                nc.gpsimd.tensor_tensor(x1b[:, t, :], x1[:, t, :], bo_sb[:], ALU.add).then_inc(s["x1b_ready"], 1)

            def st_d(t):
                pool.wait_ge(s["xinv_ready"], t + 1)
                if t >= 2:
                    pool.wait_ge(s["xp_tr"], t - 1)
                nc.gpsimd.tensor_tensor(xp[:, t % 2, :].rearrange("p (h j) -> p h j", h=XH),
                                        xe[:, t % 2, :].rearrange("p (h j) -> p h j", h=XH),
                                        xs_sum[:, t % 2, :].unsqueeze(2).to_broadcast([P, XH, CT]), ALU.mult)\
                    .then_inc(s["xp_ready"], 1)

            def st_e(t):
                pool.wait_ge(s["ln3_stats"], t + 1)
                inv_std(2, t, t + 1, "rstd3")

            for step in range(NT + 3):
                for fn, lag in ((st_b, 0), (st_d, 1), (st_e, 2)):
                    if 0 <= step - lag < NT:
                        fn(step - lag)
            pool.wait_ge(s["slot_ready"], 1)
            pool.wait_ge(s["zero_out"], 16)
            for t in range(NT):
                nc.gpsimd.indirect_dma_start(routed_dram, bass.IndirectOffsetOnAxis(ap=slot[:, t:t + 1], axis=0),
                                             xn3[:, t, :], None).then_inc(s["scattered"], 16)
            pool.wait_ge(s["y_out0"], 16 * ((NS + 1) // 2))
            pool.wait_ge(s["y_out1"], 16 * (NS // 2))
            for t in range(NT):
                nc.gpsimd.indirect_dma_start(y_back[:, t, :], None, expert_out_dram,
                                             bass.IndirectOffsetOnAxis(ap=slot[:, t:t + 1], axis=0))\
                    .then_inc(s["gathered"], 16)

        @block.vector
        def _(dve):
            chain = [0]

            def link(ins):
                chain[0] += 1
                ins.then_inc(s["dve_chain"], 1)
                dve.wait_ge(s["dve_chain"], chain[0])

            v = nc.vector

            def stats(ln, t, src, name):
                link(v.bn_stats(stat[:, ln, t, :], src))
                v.bn_aggr(mv[:, ln, t, :], stat[:, ln, t, :]).then_inc(s[name], 1)

            def normalise(dst, src, ln, t):
                return v.tensor_scalar(dst, src, mv[:, ln, t, 0:1], rstd[:, ln, t:t + 1], ALU.subtract, ALU.mult)

            for b in range(B):
                dve.wait_ge(s[f"x{b}_in"], 16)
                for t in range(b * QT, (b + 1) * QT):
                    stats(0, t, x_sb[:, t, :], "ln1_stats")
            dve.wait_ge(s["const_in"], 16)
            v.memset(ones_bf[:], 1.0)
            v.tensor_copy(cbf[:], cst[:, 0:3 * P]).then_inc(s["const_ready"], 1)
            v.memset(zeros_e[:], 0.0)
            for b in range(B):
                dve.wait_ge(s["rstd1"], b + 1)
                dve.wait_ge(s["ln1_stats"], QT * (b + 1))
                for t in range(b * QT, (b + 1) * QT):
                    normalise(xn[:, t, :], x_sb[:, t, :], 0, t).then_inc(s["xn_ready"], 1)
            for b in range(B):
                for w in range(2):
                    n = 2 * b + w
                    dve.wait_ge(s["full_ready"], n + 1)
                    dve.wait_ge(s["hi_ready"], n + 1)
                    v.tensor_tensor(rest[:, w, b, :], full[:, w, b, :], part[:, w, 0, b, :], ALU.subtract)\
                        .then_inc(s["rest_ready"], 1)
                for w in range(2):
                    n = 2 * b + w
                    dve.wait_ge(s["mid_ready"], n + 1)
                    dve.wait_ge(s["rest_ready"], n + 1)
                    v.tensor_tensor(part[:, w, 2, b, :], rest[:, w, b, :], part[:, w, 1, b, :], ALU.subtract)\
                        .then_inc(s["low_ready"], 1)
                dve.wait_ge(s["v_mm"], b + 1)
                dve.wait_ge(s["bias_in"], 32)
                v.tensor_tensor(v_sb[:, b * QT:(b + 1) * QT, :, :].rearrange("p t h d -> p t (h d)"),
                                ps[:, 1, :].rearrange("p (t n) -> p t n", t=QT),
                                b_v_sb[:, :].unsqueeze(1).to_broadcast([P, QT, D]), ALU.add)\
                    .then_inc(s["v_ready"], 1)

            def maxima(i, lo, hi):
                for u in range(lo, hi):
                    qt, j, heads = units[u]
                    dve.wait_ge(s["unit_ready"], UNITS * i + u + 1)
                    w = (qt + 1) * P
                    v.tensor_reduce(mx[:, qt, j:j + heads],
                                    bank(S_BANK[u % 2])[:, 0:heads * w].rearrange("p (h k) -> p h k", h=heads),
                                    AX.X, ALU.max).then_inc(s["unit_read"], 1)

            def max_parts(i):
                dve.wait_ge(s["unit_read"], UNITS * (i + 1))
                if i >= 1:
                    dve.wait_ge(s["m_tr"], i)
                hi, mid, low = (mparts[:, :, c, :] for c in range(3))
                link(v.tensor_scalar(hi, mx[:], -1.0, None, ALU.mult))
                link(v.scalar_tensor_tensor(out=mrest[:], in0=mx[:], scalar=-1.0, in1=hi, op0=ALU.mult,
                                            op1=ALU.subtract))
                link(v.tensor_copy(mid, mrest[:]))
                v.tensor_tensor(low, mrest[:], mid, ALU.subtract).then_inc(s["mparts_ready"], 1)

            def attn_out(i):
                dve.wait_ge(s["o_tr"], i + 1)
                o = bank(MISC).rearrange("p (t h w) -> p t h w", t=QT, h=GH)
                link(v.reciprocal(den[:], o[:, :, :, DH]))
                b, g = i // GPB, i % GPB
                v.tensor_tensor(attn[:, b * QT:(b + 1) * QT, GH * g:GH * (g + 1), :], o[:, :, :, 0:DH],
                                den[:].unsqueeze(3).to_broadcast([P, QT, GH, DH]), ALU.mult)\
                    .then_inc(s["attn_ready"], 1)

            for i in range(2):
                maxima(i, 0, UNITS)
                max_parts(i)
            for i in range(NG + 1):
                if i + 2 < NG:
                    maxima(i + 2, 0, 6)
                if i >= 1:
                    attn_out(i - 1)
                if i + 2 < NG:
                    maxima(i + 2, 6, UNITS)
                    max_parts(i + 2)

            def st_b(t):
                dve.wait_ge(s["x1_mm"], t + 1)
                if t == 0:
                    dve.wait_ge(s["xb_ready"], 1)
                v.tensor_tensor(x1[:, t, :], bank(2)[:, 0:P], xb[:, t, :], ALU.add).then_inc(s["x1_ready"], 1)
                dve.wait_ge(s["x1_ready"], t + 1)
                stats(1, t, x1[:, t, :], "ln2_stats")

            def st_c(t):
                dve.wait_ge(s["rstd2"], t + 1)
                dve.wait_ge(s["ln2_stats"], t + 1)
                if t >= 2:
                    dve.wait_ge(s["xn2_tr"], t - 1)
                normalise(xn2[:, t % 2, :], x1[:, t, :], 1, t).then_inc(s["xn2_ready"], 1)

            def st_d(t):
                dve.wait_ge(s["xs_mm"], t + 1)
                sc = bank(6 + t % 2).rearrange("p (h j) -> p h j", h=XH)
                link(v.tensor_reduce(xm[:, t % 2, :], sc, AX.X, ALU.max))
                if t >= 2:
                    dve.wait_ge(s["xp_ready"], t - 1)
                v.tensor_tensor(xe[:, t % 2, :].rearrange("p (h j) -> p h j", h=XH), sc,
                                xm[:, t % 2, :].unsqueeze(2).to_broadcast([P, XH, CT]), ALU.subtract)\
                    .then_inc(s["xsub_ready"], 1)

            def st_d2(t):
                dve.wait_ge(s["xexp_done"], t + 1)
                link(v.tensor_reduce(xs_sum[:, t % 2, :], xe[:, t % 2, :].rearrange("p (h j) -> p h j", h=XH),
                                     AX.X, ALU.add))
                v.reciprocal(xs_sum[:, t % 2, :], xs_sum[:, t % 2, :]).then_inc(s["xinv_ready"], 1)

            def st_e(t):
                dve.wait_ge(s["x2_mm"], t + 1)
                dve.wait_ge(s["x1b_ready"], t + 1)
                v.tensor_tensor(x2[:, t, :], bank(3)[:, 0:P], x1b[:, t, :], ALU.add).then_inc(s["x2_ready"], 1)
                dve.wait_ge(s["x2_ready"], t + 1)
                stats(2, t, x2[:, t, :], "ln3_stats")

            def st_e2(t):
                dve.wait_ge(s["rstd3"], t + 1)
                dve.wait_ge(s["ln3_stats"], t + 1)
                normalise(xn3[:, t, :], x2[:, t, :], 2, t).then_inc(s["xn3_ready"], 1)

            for step in range(NT + 4):
                for fn, lag in ((st_b, 0), (st_c, 0), (st_d, 1), (st_d2, 1), (st_e, 2), (st_e2, 2)):
                    if 0 <= step - lag < NT:
                        fn(step - lag)

            dve.wait_ge(s["logits_mm"], NT)
            lg = bank(5)[:, 0:NT * E].rearrange("p (t e) -> p t e", t=NT)

            def over_e(ap):
                return ap.unsqueeze(2).to_broadcast([P, NT, E])

            def over_t(ap):
                return ap.unsqueeze(1).to_broadcast([P, NT, E])

            link(v.tensor_reduce(logit_max[:], lg, AX.X, ALU.max))
            link(v.tensor_tensor(first[:], lg, over_e(logit_max[:]), ALU.is_equal))
            link(v.tensor_tensor(first[:], first[:], over_t(first_rank), ALU.mult))
            link(v.tensor_reduce(first_max[:], first[:], AX.X, ALU.max))
            link(v.tensor_tensor(chosen[:], first[:], over_e(first_max[:]), ALU.is_equal))
            v.tensor_copy(chosen_bf[:], chosen[:]).then_inc(s["chosen_ready"], 1)
            dve.wait_ge(s["counts_mm"], 1)
            cnt = bank(6)[:, 0:E]
            link(v.tensor_tensor(over[:], cnt.unsqueeze(2).to_broadcast([P, E, NT]), tile_edges, ALU.is_gt))
            link(v.tensor_reduce(expert_tiles[:], over[:], AX.X, ALU.add))
            link(v.tensor_tensor_scan(tiles_end[:], expert_tiles[:], zeros_e[:], 0.0, ALU.add, ALU.add))
            link(v.tensor_tensor(run_start[:], tiles_end[:], expert_tiles[:], ALU.subtract))
            link(v.tensor_scalar(run_start[:], run_start[:], float(P), None, ALU.mult))
            rank = bank(7)[:, 0:NT * E].rearrange("p (t e) -> p t e", t=NT)
            link(v.tensor_tensor(slot_e[:], rank, over_t(run_start[:]), ALU.add))
            link(v.tensor_tensor(slot_e[:], slot_e[:], chosen[:], ALU.mult))
            link(v.tensor_reduce(slot_f[:], slot_e[:], AX.X, ALU.add))
            dve.wait_ge(s["xn3_ready"], NT)
            v.tensor_copy(slot[:], slot_f[:]).then_inc(s["slot_ready"], 1)
            link(v.tensor_tensor(past[:], tiles_end[:].unsqueeze(1).to_broadcast([P, NS, E]), tile_index, ALU.is_le))
            link(v.tensor_reduce(tile_expert_f[:, 0, :], past[:], AX.X, ALU.add))
            link(v.tensor_scalar(tile_expert_f[:, 1, :], tile_expert_f[:, 0, :], float(E - 1), float(IC * D),
                                 ALU.min, ALU.mult))
            link(v.tensor_scalar(tile_expert_f[:, 0, :], tile_expert_f[:, 0, :], float(E - 1), float(2 * I),
                                 ALU.min, ALU.mult))
            v.tensor_copy(tile_expert[:], tile_expert_f[:]).then_inc(s["experts_known"], 1)

            def mx_b(n):
                dve.wait_ge(s["silu_done"], n + 1)
                dve.wait_ge(s["up_mm"], n + 1)
                if n >= 2:
                    dve.wait_ge(s["hidden_tr"], n - 1)
                v.tensor_tensor(hidden[:, n % 2, :], bank(3 + n % 2)[:, 0:I], act_gate[:, n % 2, :], ALU.mult)\
                    .then_inc(s["hidden_ready"], 1)

            def mx_d(n):
                dve.wait_ge(s["y_mm"], n + 1)
                if n >= 2:
                    dve.wait_ge(s[f"y_out{n % 2}"], 16 * (n // 2))
                v.tensor_copy(y_sb[:, n % 2, :], bank(6 + n % 2)[:, 0:D]).then_inc(s["y_ready"], 1)

            for step in range(NS + 3):
                for fn, lag in ((mx_b, 1), (mx_d, 3)):
                    if 0 <= step - lag < NS:
                        fn(step - lag)
            dve.wait_ge(s["gathered"], 16 * NT)
            for t in range(NT):
                v.tensor_tensor(res[:, t, :], x2[:, t, :], y_back[:, t, :], ALU.add).then_inc(s["res_ready"], 1)

        @block.tensor
        def _(pe):
            def mm(o, lhs, rhs, start=True, stop=True):
                return nc.tensor.matmul(o, lhs, rhs, start=start, stop=stop)

            pe.wait_ge(s["ctx_in"], 16)
            pe.wait_ge(s["wkv_in"], 32)
            for w, (name, wt) in enumerate((("kt_mm", wk_sb), ("vt_mm", wv_sb))):
                for c in range(XC):
                    last = mm(bank(4 + w)[:, c * B * CT:(c + 1) * B * CT], wt[:, c * P:(c + 1) * P], ctx_sb[:])
                last.then_inc(s[name], 1)
            pe.wait_ge(s["const_in"], 16)
            for b in range(B):
                for t in range(QT):
                    n = b * QT + t
                    pe.wait_ge(s["xn_ready"], n + 1)
                    last = nc.tensor.transpose(bank(b)[:, t * P:(t + 1) * P], xn[:, n, :], ident)
                last.then_inc(s["xn_tr"], 1)
            pe.wait_ge(s["w_attn_in"], 16)
            for b in range(B):
                pe.wait_ge(s["xn_t_ready"], b + 1)
                for w in range(2):
                    if b >= 1:
                        pe.wait_ge(s["hi_ready"], w + 1)
                    mm(bank(2 + w), w_attn_sb[:, w * D:(w + 1) * D], xn_t[:, b, :]).then_inc(s["qk_mm"], 1)
                if b >= 1:
                    pe.wait_ge(s["v_ready"], b)
                else:
                    pe.wait_ge(s["xn_t_ready"], 2)
                for t in range(QT):
                    last = mm(bank(1)[:, t * D:(t + 1) * D], xn_t[:, b, t * P:(t + 1) * P], w_attn_sb[:, 2 * D:3 * D])
                last.then_inc(s["v_mm"], 1)
            pe.wait_ge(s["wqo_in"], 32)
            pe.wait_ge(s["kt_read"], 2)
            for c in range(XC):
                last = mm(bank(6 + c // 4)[:, (c % 4) * P:(c % 4 + 1) * P], wq_sb[:, c, :],
                          k_blk[:, c].rearrange("p b h j -> p (b h j)"))
                if c % 4 == 3:
                    last.then_inc(s["a_mm"], 1)
            pe.wait_ge(s["vt_read"], 2)
            for b in range(B):
                for c in range(XC):
                    rows = slice(64 * (c % 2), 64 * (c % 2) + 64)
                    last = mm(ps[rows, 4 + b, (c // 2) * D:(c // 2 + 1) * D],
                              v_blk[:, c, b].rearrange("p h j -> p (h j)"), wo_sb[:, c, :])
            last.then_inc(s["bm_mm"], 1)

            def scores(i, lo, hi):
                for u in range(lo, hi):
                    qt, j0, heads = units[u]
                    w = (qt + 1) * P
                    n = UNITS * i + u
                    if n >= 2:
                        pe.wait_ge(s["unit_read"], n - 1)
                    for j in range(heads):
                        hh = GH * i + j0 + j
                        o = bank(S_BANK[u % 2])[:, j * w:(j + 1) * w]
                        mm(o, qs[0:SC, hh, qt * P:(qt + 1) * P], ks[0:SC, hh, 0:w], stop=False)
                        last = mm(o[:, qt * P:w], ident_bf, causal_bf, start=False)
                    last.then_inc(s["unit_ready"], 1)

            def max_transposes(i):
                pe.wait_ge(s["mparts_ready"], i + 1)
                if i >= 3:
                    pe.wait_ge(s["attn_ready"], i - 2)
                for qt in range(QT):
                    last = nc.tensor.transpose(bank(MISC)[0:3 * GH, qt * P // 2:(qt + 1) * P // 2].bitcast(BF16),
                                               mparts[:, qt].rearrange("p c h -> p (c h)"), ident_bf)
                last.then_inc(s["m_tr"], 1)

            def scores_t(i, kt):
                if kt == 0:
                    pe.wait_ge(s["m_rows_odd" if i % 2 else "m_rows_even"], 48 * (i // 2 + 1))
                for pair in range(2):
                    u = KU * i + 2 * kt + pair
                    if u >= 2:
                        pe.wait_ge(s["exp_done"], u - 1)
                    for j in range(2):
                        hh = GH * i + 2 * pair + j
                        last = mm(bank(ST_BANK[pair] + j)[:, kt * P:T], ks[0:SA, hh, kt * P:(kt + 1) * P],
                                  qs[0:SA, hh, kt * P:T])
                    last.then_inc(s["st_ready"], 1)

            def weighted(i, kt):
                pe.wait_ge(s["masked"], KU * i + 2 * kt + 2)
                pe.wait_ge(s["vg_ready"], QT * i + kt + 1)
                if kt == 0 and i >= 1:
                    pe.wait_ge(s["o_copied"], i)
                for j in range(GH):
                    last = mm(ps[VW * j:VW * (j + 1), O_BANK, kt * P:T], vg[:, kt, j, :], probs[:, kt, j, kt * P:T],
                              start=(kt == 0), stop=(kt == QT - 1))
                last.then_inc(s["pv_done"], 1)

            def o_transposes(i):
                pe.wait_ge(s["o_copied"], i + 1)
                pe.wait_ge(s["m_t_ready"], min(i + 3, NG))
                if i >= 1:
                    pe.wait_ge(s["attn_ready"], i)
                for qt in range(QT):
                    last = nc.tensor.transpose(bank(MISC)[:, qt * P:(qt + 1) * P], o_sb[:, qt * P:(qt + 1) * P], ident)
                last.then_inc(s["o_tr"], 1)

            pe.wait_ge(s["const_ready"], 1)
            pe.wait_ge(s["v_ready"], B)
            pe.wait_ge(s["stack0_in"], 16 * 18)
            pe.wait_ge(s["a_read"], 2)
            scores(0, 0, UNITS)
            max_transposes(0)
            scores(1, 0, UNITS)
            pe.wait_ge(s["ones_in"], 16)
            pe.wait_ge(s["bm_read"], 1)
            for i in range(NG + 1):
                if i + 2 == GPB:
                    pe.wait_ge(s["stack1_in"], 16 * 18)
                if i < NG:
                    scores_t(i, 0)
                if i >= 1:
                    weighted(i - 1, QT - 1)
                if i + 2 < NG:
                    scores(i + 2, 0, 3)
                if i + 1 < NG:
                    max_transposes(i + 1)
                if i < NG:
                    scores_t(i, 1)
                    weighted(i, 0)
                if i + 2 < NG:
                    scores(i + 2, 3, 6)
                if i >= 1:
                    o_transposes(i - 1)
                if i < NG:
                    scores_t(i, 2)
                    weighted(i, 1)
                if i + 2 < NG:
                    scores(i + 2, 6, 9)
                if i < NG:
                    scores_t(i, 3)
                    weighted(i, 2)
                if i + 2 < NG:
                    scores(i + 2, 9, UNITS)

            pe.wait_ge(s["proj_in"], 16)

            def st_a(t):
                if t == 0:
                    pe.wait_ge(s["attn_ready"], NG)
                if t >= 1:
                    pe.wait_ge(s["attn_t_ready"], t)
                nc.tensor.transpose(bank(0)[:, 0:P], attn[:, t].rearrange("p h d -> p (h d)"), ident)\
                    .then_inc(s["attn_tr"], 1)
                pe.wait_ge(s["attn_t_ready"], t + 1)
                if t >= 1:
                    pe.wait_ge(s["x1_ready"], t)
                mm(bank(2)[:, 0:D], tr_sb[:, 0, :], w_proj_sb[:]).then_inc(s["x1_mm"], 1)

            def st_c(t):
                pe.wait_ge(s["xn2_ready"], t + 1)
                if t >= 4:
                    pe.wait_ge(s["xn3_t_ready"], t - 3)
                if t >= 1:
                    pe.wait_ge(s["xn2_t_ready"], t)
                nc.tensor.transpose(bank(1)[:, 0:P], xn2[:, t % 2, :], ident).then_inc(s["xn2_tr"], 1)
                pe.wait_ge(s["xn2_t_ready"], t + 1)
                if t >= 2:
                    pe.wait_ge(s["xsub_ready"], t - 1)
                mm(bank(6 + t % 2), tr_sb[:, 1, :], a_sb[:, t // QT, :]).then_inc(s["xs_mm"], 1)

            def st_e(t):
                pe.wait_ge(s["xp_ready"], t + 1)
                if t >= 1:
                    pe.wait_ge(s["xp_t_ready"], t)
                for c in range(4):
                    last = nc.tensor.transpose(bank(4)[:, c * P:(c + 1) * P], xp[:, t % 2, c * P:(c + 1) * P], ident)
                last.then_inc(s["xp_tr"], 1)
                pe.wait_ge(s["xp_t_ready"], t + 1)
                if t >= 1:
                    pe.wait_ge(s["x2_ready"], t)
                for c in range(4):
                    last = mm(bank(3)[:, 0:D], xp_t[:, t % 2, c * P:(c + 1) * P], bm_sb[:, t // QT, c, :],
                              start=(c == 0), stop=(c == 3))
                last.then_inc(s["x2_mm"], 1)

            def st_f(t):
                pe.wait_ge(s["xn3_ready"], t + 1)
                pe.wait_ge(s["xn2_t_ready"], min(t + 4, NT))
                if t >= 1:
                    pe.wait_ge(s["xn3_t_ready"], t)
                nc.tensor.transpose(bank(1)[:, P:2 * P], xn3[:, t, :], ident).then_inc(s["xn3_tr"], 1)
                pe.wait_ge(s["xn3_t_ready"], t + 1)
                if t == 0:
                    pe.wait_ge(s["router_in"], 16)
                mm(bank(5)[:, t * E:(t + 1) * E], tr_sb[:, 2, :], router_sb[:]).then_inc(s["logits_mm"], 1)

            for step in range(NT + 3):
                for fn, lag in ((st_a, 0), (st_c, 0), (st_e, 2), (st_f, 3)):
                    if 0 <= step - lag < NT:
                        fn(step - lag)

            pe.wait_ge(s["chosen_ready"], 1)
            pe.wait_ge(s["xsub_ready"], NT)
            for t in range(NT):
                last = mm(bank(6)[:, 0:E], ones_bf[:], chosen_bf[:, t, :], start=(t == 0), stop=(t == NT - 1))
            mm(bank(7)[:, 0:NT * E], before_bf, chosen_bf[:].rearrange("p t e -> p (t e)"), stop=False)
            for back in range(1, NT):
                last = mm(bank(7)[:, back * E:NT * E], ones_bf[:],
                          chosen_bf[:, 0:NT - back].rearrange("p t e -> p (t e)"), start=False, stop=(back == NT - 1))
            last.then_inc(s["counts_mm"], 1)

            pe.wait_ge(s["experts_in"], 32)
            pe.wait_ge(s["experts_known"], 1)

            def mx_a(n):
                pe.wait_ge(s["routed_in"], 16 * 3)
                if n >= 1:
                    pe.wait_ge(s["routed_t_ready"], n)
                nc.tensor.transpose(bank(0)[:, 0:P], routed[:, n, :], ident).then_inc(s["routed_tr"], 1)

            def mx_b(n):
                off = pe.value_load(tile_expert[0:1, 0, n:n + 1], min_val=0, max_val=(E - 1) * 2 * I)
                pe.wait_ge(s["routed_t_ready"], n + 1)
                if n >= 2:
                    pe.wait_ge(s["silu_done"], n - 1)
                mm(bank(1 + n % 2)[:, 0:I], routed_t[:, n % 2, :], gate_up_sb[:, bass.ds(off, I)])\
                    .then_inc(s["gate_mm"], 1)
                if n >= 2:
                    pe.wait_ge(s["hidden_ready"], n - 1)
                mm(bank(3 + n % 2)[:, 0:I], routed_t[:, n % 2, :], gate_up_sb[:, bass.ds(off + I, I)])\
                    .then_inc(s["up_mm"], 1)

            def mx_c(n):
                pe.wait_ge(s["hidden_ready"], n + 1)
                if n >= 1:
                    pe.wait_ge(s["hidden_t_ready"], n)
                nc.tensor.transpose(bank(5)[:, 0:P], hidden[:, n % 2, 0:P], ident)
                nc.tensor.transpose(bank(5)[:, P:2 * P], hidden[:, n % 2, P:2 * P], ident)
                nc.tensor.transpose(bank(5)[0:IR, 2 * P:3 * P], hidden[:, n % 2, 2 * P:I], ident)\
                    .then_inc(s["hidden_tr"], 1)

            def mx_d(n):
                off = pe.value_load(tile_expert[0:1, 1, n:n + 1], min_val=0, max_val=(E - 1) * IC * D)
                pe.wait_ge(s["hidden_t_ready"], n + 1)
                if n >= 2:
                    pe.wait_ge(s["y_ready"], n - 1)
                o = bank(6 + n % 2)[:, 0:D]
                mm(o, hidden_t[:, n % 2, 0, :], down_sb[:, bass.ds(off, D)], stop=False)
                mm(o, hidden_t[:, n % 2, 1, :], down_sb[:, bass.ds(off + D, D)], start=False, stop=False)
                mm(o, hidden_t[0:IR, n % 2, 2, :], down_sb[0:IR, bass.ds(off + 2 * D, D)], start=False)\
                    .then_inc(s["y_mm"], 1)

            for step in range(NS + 3):
                for fn, lag in ((mx_a, 0), (mx_b, 1), (mx_c, 2), (mx_d, 3)):
                    if 0 <= step - lag < NS:
                        fn(step - lag)


def kernel(**inputs):
    import numpy as _np
    import concourse.bacc as _bacc
    from concourse import mybir as _mybir
    from concourse.bass_utils import run_bass_kernel_spmd as _run

    a = {k: _np.asarray(v) for k, v in inputs.items()}
    consts = _np.zeros((P, CONST_W), _np.float32)
    r = _np.arange(P)
    consts[:, 0:P] = r[:, None] == r[None, :]
    consts[:, P:2 * P] = _np.where(r[None, :] <= r[:, None], 0.0, -1e30)
    consts[:, 2 * P:3 * P] = r[:, None] < r[None, :]
    o0 = 3 * P
    consts[:, o0:o0 + E * NT] = _np.tile(P * _np.arange(NT), E)
    o0 += E * NT
    consts[:, o0:o0 + NS * E] = _np.repeat(_np.arange(NS), E)
    consts[:, o0 + NS * E:] = E - _np.arange(E)
    down = a["L0_ffn_down_w"].transpose(0, 2, 1)
    down = _np.concatenate([down, _np.zeros((E, IC * P - I, D), down.dtype)], axis=1)
    b_attn = a["L0_attn_b_attn"]
    arrays = {
        "x": a["x"],
        "ctx_t": a["ctx_768"].transpose(2, 0, 1).reshape(CW, B * CT),
        "w_attn": a["L0_attn_W_attn"],
        "b_attn_qk": b_attn[0:2 * D].reshape(2, D).T,
        "b_attn_v": b_attn[2 * D:3 * D],
        "w_proj": a["L0_attn_W_proj"],
        "b_proj": a["L0_attn_b_proj"],
        "wq_t": a["L0_xattn_Wq"].T,
        "wk": a["L0_xattn_Wk"],
        "wv": a["L0_xattn_Wv"],
        "wo": a["L0_xattn_Wo"],
        "bo": a["L0_xattn_bo"],
        "router_t": a["L0_ffn_router_w"].T,
        "gate_up": _np.stack([a["L0_ffn_gate_w"], a["L0_ffn_up_w"]], axis=1)
                      .transpose(3, 0, 1, 2).reshape(D, E * 2 * I),
        "down": down.reshape(E, IC, P, D).transpose(2, 0, 1, 3).reshape(P, E * IC * D),
        "consts": consts,
    }
    nc = _bacc.Bacc("TRN2", target_bir_lowering=False, num_devices=1)
    feed, args = {}, {}
    for name, v in arrays.items():
        v = _np.ascontiguousarray(v)
        feed[f"in_{name}"] = v
        args[name] = nc.dram_tensor(f"in_{name}", v.shape, _mybir.dt.from_np(v.dtype), kind="ExternalInput").ap()
    out = nc.dram_tensor("out_0", (B, T, D), F32, kind="ExternalOutput").ap()
    decoder_layer(nc, out=out, **args)
    got = _run(nc, [feed], core_ids=[0])
    return got.results[0]["out_0"]
```

```python
from contextlib import ExitStack

import concourse.bass as bass
from concourse import mybir

F32 = mybir.dt.float32
BF16 = mybir.dt.bfloat16
I32 = mybir.dt.int32
ALU = mybir.AluOpType
ACT = mybir.ActivationFunctionType
AX = mybir.AxisListType

P = 128
B, T, D = 2, 512, 128
QT = T // P
NT = B * QT
H, DH = 16, 8
GH = 4
NG = B * H // GH
GPB = H // GH
SC = 9 * DH
MP = 2
SA = SC + MP
VW = 32
CT, CW = 32, 96
XH, XD = 16, 64
XC = XH * XD // P
XS = XH * CT
E, I = 8, 352
IC = 3
IR = I - 2 * P
PW = 2 * D + 1
NS = (NT * P + E * (P - 1)) // P
READS = ((0, 1), (1, 3), (3, 7), (7, NS))
WARM = 12
YB = 4
EPS = 1e-5
UNITS = 12
KU = 2 * QT
CONST_W = 3 * P + E * NT + NS * E + E + NT

SPLIT = {"q": 0, "k": 1}


def max_units():
    units = []
    for qt in reversed(range(QT)):
        heads = {3: 1, 2: 1, 1: 2, 0: 2}[qt]
        units += [(qt, j, heads) for j in range(0, GH, heads)]
    return units


def decoder_layer(nc, x, ctx_t, w_attn, b_attn_qk, b_attn_v, w_proj, b_proj, wq_t, wk, wv, wo, bo,
                  router_t, gate_up, down, consts, out):
    units = max_units()
    assert len(units) == UNITS

    with ExitStack() as ctx:
        def sb(name, shape, dt=F32):
            return ctx.enter_context(nc.sbuf_tensor(name, shape, dt))

        def sem(name):
            return ctx.enter_context(nc.semaphore(name))

        q_parts_dram = nc.dram_tensor("q_parts_dram", (B, H, 3, DH, T), BF16, kind="Internal").ap()
        k_parts_dram = nc.dram_tensor("k_parts_dram", (B, H, 5, DH, T), BF16, kind="Internal").ap()
        routed_dram = nc.dram_tensor("routed_dram", (NS * P, PW), F32, kind="Internal").ap()

        cst = sb("cst", [P, CONST_W])
        ident = cst[:, 0:P]
        o0 = 3 * P
        tile_edges = cst[:, o0:o0 + E * NT].rearrange("p (e k) -> p e k", e=E)
        o0 += E * NT
        tile_index = cst[:, o0:o0 + NS * E].rearrange("p (s e) -> p s e", s=NS)
        first_rank = cst[:, o0 + NS * E:o0 + NS * E + E]
        token_number = cst[:, CONST_W - NT:CONST_W]
        cbf = sb("cbf", [P, 3 * P], BF16)
        ident_bf, causal_bf, before_bf = cbf[:, 0:P], cbf[:, P:2 * P], cbf[:, 2 * P:3 * P]
        ones_bf = sb("ones_bf", [P, P], BF16)
        ones_row = sb("ones_row", [MP, T], BF16)
        neg_half = sb("neg_half", [P, NT])
        w_attn_sb = sb("w_attn_sb", [P, 3 * D])
        b_qk_sb = sb("b_qk_sb", [P, 2])
        b_v_sb = sb("b_v_sb", [P, D])
        w_proj_sb = sb("w_proj_sb", [P, D])
        b_proj_sb = sb("b_proj_sb", [P, D])
        bo_sb = sb("bo_sb", [P, D])
        ctx_sb = sb("ctx_sb", [CW, B * CT])
        router_sb = sb("router_sb", [P, E])

        x_sb = sb("x_sb", [P, NT, D])
        xb = sb("xb", [P, NT, D])
        xn = sb("xn", [P, NT, D])
        xn_t = sb("xn_t", [P, B, T])
        stat = sb("stat", [P, 3, NT, 6])
        mv = sb("mv", [P, 3, NT, 2])
        var_eps = sb("var_eps", [P, 3, NT])
        rstd = sb("rstd", [P, 3, NT])
        part = sb("part", [P, 2, 3, B, T], BF16)
        qs = sb("qs", [P, B * H, T], BF16)
        ks = sb("ks", [P, B * H, T], BF16)
        gate_up_sb = qs[:].rearrange("p h t -> p (h t)").bitcast(F32)[:, 0:E * 2 * I]
        down_sb = ks[:].rearrange("p h t -> p (h t)").bitcast(F32)[:, 0:E * IC * D]
        v_sb = sb("v_sb", [P, NT, H, DH])
        vg = sb("vg", [P, QT, GH, VW])
        mx = sb("mx", [P, 2, QT, GH])
        mparts = sb("mparts", [P, QT, MP, GH], BF16)
        m_t = sb("m_t", [MP * GH, T], BF16)
        probs = sb("probs", [P, QT, GH, T])
        room = probs[:].rearrange("p a h t -> p (a h t)")
        full = room[:, 0:2 * B * T].rearrange("p (w b t) -> p w b t", w=2, b=B)
        rest = room[:, 2 * B * T:4 * B * T].rearrange("p (w b t) -> p w b t", w=2, b=B)
        o0, n = 4 * B * T, XH * XD
        wk_sb = room[0:CW, o0:o0 + n]
        wv_sb = room[0:CW, o0 + n:o0 + 2 * n]
        wq_sb = room[:, o0 + 2 * n:o0 + 3 * n].rearrange("p (c d) -> p c d", c=XC)
        wo_sb = room[:, o0 + 3 * n:o0 + 4 * n].rearrange("p (c d) -> p c d", c=XC)
        routed = room[:, 0:NS * PW].rearrange("p (n w) -> p n w", n=NS)
        o0 = NS * PW
        y_sb = room[:, o0:o0 + YB * D].rearrange("p (n d) -> p n d", n=YB)
        o0 += YB * D
        hidden_t = room[:, o0:o0 + 2 * IC * P].rearrange("p (n c q) -> p n c q", n=2, c=IC)
        o_sb = sb("o_sb", [P, T])
        attn = sb("attn", [P, NT, H, DH])
        den = sb("den", [P, QT, GH])
        k_blk = sb("k_blk", [P, XC, B, 2, CT])
        v_blk = sb("v_blk", [P, XC, B, 2, CT])
        a_sb = sb("a_sb", [P, B, XS])
        bm_sb = sb("bm_sb", [P, B, 4, D])
        tr_sb = sb("tr_sb", [P, 4, P])
        x1 = sb("x1", [P, NT, D])
        x1b = sb("x1b", [P, NT, D])
        xn2 = sb("xn2", [P, 2, D])
        xm = sb("xm", [P, 2, XH])
        xe = sb("xe", [P, 2, XS])
        xp = sb("xp", [P, 2, XS])
        xs_sum = sb("xs_sum", [P, 2, XH])
        xp_t = sb("xp_t", [P, 2, XS])
        row = sb("row", [P, NT, PW])
        xn3, x2 = row[:, :, 0:D], row[:, :, D:2 * D]
        row_token = row[:, :, 2 * D].bitcast(I32)
        logit_max = sb("logit_max", [P, NT])
        first = sb("first", [P, NT, E])
        first_max = sb("first_max", [P, NT])
        chosen = sb("chosen", [P, NT, E])
        chosen_bf = sb("chosen_bf", [P, NT, E], BF16)
        over = sb("over", [P, E, NT])
        expert_tiles = sb("expert_tiles", [P, E])
        zeros_e = sb("zeros_e", [P, E])
        tiles_end = sb("tiles_end", [P, E])
        run_start = sb("run_start", [P, E])
        slot_e = sb("slot_e", [P, NT, E])
        slot_f = sb("slot_f", [P, NT])
        slot = sb("slot", [P, NT], I32)
        past = sb("past", [P, NS, E])
        tile_expert_f = sb("tile_expert_f", [P, 2, NS])
        tile_expert = sb("tile_expert", [P, 2, NS], I32)
        empty_row = sb("empty_row", [P, PW])
        routed_t = sb("routed_t", [P, 2, P])
        act_gate = sb("act_gate", [P, 2, I])
        hidden = sb("hidden", [P, 2, I])

        warm = sb("warm", [P, T], BF16)
        warm_act = sb("warm_act", [P, 1])

        ps = ctx.enter_context(nc.psum_tensor("ps", [P, 8, T], F32))

        names = """x0_in x1_in warm_ready ln1_sums w_attn_in bias_in const_in ctx_in wkv_in wqo_in proj_in xbias_in router_in experts_in
            const_ready ones_ready dve_chain act_chain pool_chain pe_chain
            ln1_stats rstd1 xn_ready xn_tr xn_t_ready qk_mm qk_read v_mm v_ready
            full_ready hi_ready rest_ready mid_ready low_ready parts_out0 parts_out1 stack0_first stack0_in stack1_first stack1_in ones_in
            kt_mm kt_read vt_mm vt_read kv_blk_zero a_mm a_read bm_mm bm_read
            unit_ready unit_read mparts_ready m_tr m_t_ready m_rows_even m_rows_odd
            st_ready exp_done masked v_copied pv_done o_copied o_tr attn_ready
            attn_tr attn_t_ready x1_mm x1_ready x1b_ready ln2_stats rstd2 xn2_ready xn2_tr xn2_t_ready
            xs_mm ln2_sums ln3_sums xmax_ready xsum_ready xsub_ready xexp_done xinv_ready xp_ready xp_tr xp_t_ready x2_mm x2_ready
            ln3_stats rstd3 xn3_ready xn3_tr xn3_t_ready logits_mm chosen_ready counts_mm counts_read slot_ready
            experts_known zero_ready zero_out scattered routed_in0 routed_in1 routed_in2 routed_in3 routed_tr routed_t_ready
            gate_mm up_mm silu_done hidden_ready hidden_tr hidden_t_ready y_mm y_ready out_done0 out_done1 out_done2 out_done3
            tokens_ready vg_ready xb_ready""".split()
        s = {n: sem(n) for n in names}

        block = ctx.enter_context(nc.Block())

        def bank(n):
            return ps[:, n, :]

        S_BANK = (0, 1)
        ST_BANK = (2, 4)
        O_BANK = 6
        MISC = 7

        @block.sync
        def _(sp):
            sp.dma_start(x_sb[:, 0:QT, :], x[0].rearrange("(t p) d -> p t d", p=P)).then_inc(s["x0_in"], 16)
            sp.dma_start(cst[:], consts).then_inc(s["const_in"], 16)
            sp.dma_start(w_attn_sb[:], w_attn).then_inc(s["w_attn_in"], 16)
            sp.dma_start(x_sb[:, QT:NT, :], x[1].rearrange("(t p) d -> p t d", p=P)).then_inc(s["x1_in"], 16)
            sp.dma_start(ctx_sb[:], ctx_t).then_inc(s["ctx_in"], 16)
            sp.dma_start(wk_sb, wk).then_inc(s["wkv_in"], 16)
            sp.dma_start(wv_sb, wv).then_inc(s["wkv_in"], 16)
            sp.dma_start(wq_sb, wq_t.rearrange("(c p) d -> p c d", p=P)).then_inc(s["wqo_in"], 16)
            sp.dma_start(wo_sb, wo.rearrange("(c p) d -> p c d", p=P)).then_inc(s["wqo_in"], 16)
            for b in range(B):
                out_sem = s[f"parts_out{b}"]
                for p, ready in enumerate(("hi_ready", "mid_ready", "low_ready")):
                    for w, dst, places in ((0, q_parts_dram, (p,)), (1, k_parts_dram, (p, p + 3)[:2 if p < 2 else 1])):
                        sp.wait_ge(s[ready], 2 * b + w + 1)
                        for place in places:
                            sp.dma_start(dst[b, :, place], part[:, w, p, b, :]).then_inc(out_sem, 16)
                sp.wait_ge(out_sem, 16 * 8)
                for h0, h1, in_sem in ((0, GH, s[f"stack{b}_first"]), (GH, H, s[f"stack{b}_in"])):
                    for r in range(3):
                        rows, hs = slice(r * 3 * DH, (r + 1) * 3 * DH), slice(b * H + h0, b * H + h1)
                        sp.dma_start(qs[rows, hs, :],
                                     q_parts_dram[b, h0:h1].rearrange("h c d t -> (c d) h t"))\
                            .then_inc(in_sem, 16)
                        sp.dma_start(ks[rows, hs, :],
                                     k_parts_dram[b, h0:h1, r:r + 3].rearrange("h c d t -> (c d) h t"))\
                            .then_inc(in_sem, 16)
            for i in range(NG):
                sp.wait_ge(s["m_t_ready"], i + 1)
                n0, n1 = 2 * i, min(2 * i + 2, NS)
                for c in range(MP):
                    sp.dma_start(qs[SC + c:SC + c + 1, GH * i:GH * (i + 1), :],
                                 m_t[GH * c:GH * (c + 1), :]).then_inc(s["m_rows_odd" if i % 2 else "m_rows_even"], 16)
                if i == 0:
                    sp.wait_ge(s["zero_ready"], 2)
                sp.dma_start(routed_dram[n0 * P:n1 * P].rearrange("(s p) d -> p s d", p=P),
                             empty_row[:, :].unsqueeze(1).to_broadcast([P, n1 - n0, PW])).then_inc(s["zero_out"], 16)
            sp.wait_ge(s["st_ready"], KU * NG)
            sp.dma_start(gate_up_sb, gate_up).then_inc(s["experts_in"], 16)
            sp.dma_start(down_sb, down).then_inc(s["experts_in"], 16)
            sp.wait_ge(s["scattered"], 16 * NT)
            for c, (n0, n1) in enumerate(READS):
                sp.dma_start(routed[:, n0:n1, :],
                             routed_dram[n0 * P:n1 * P].rearrange("(s p) d -> p s d", p=P))\
                    .then_inc(s[f"routed_in{c}"], 16)

        @block.scalar
        def _(act):
            def copy(dst, src):
                return nc.scalar.activation(dst, src, ACT.Copy)

            act.dma_start(b_qk_sb[:], b_attn_qk).then_inc(s["bias_in"], 16)
            act.dma_start(b_v_sb[:], b_attn_v.partition_broadcast(P)).then_inc(s["bias_in"], 16)
            act.dma_start(w_proj_sb[:], w_proj).then_inc(s["proj_in"], 16)
            act.dma_start(b_proj_sb[:], b_proj.partition_broadcast(P)).then_inc(s["xbias_in"], 16)
            act.dma_start(bo_sb[:], bo.partition_broadcast(P)).then_inc(s["xbias_in"], 16)
            act.dma_start(router_sb[:], router_t).then_inc(s["router_in"], 16)
            act.wait_ge(s["ones_ready"], 1)
            act.dma_start(ks[SC:SA, :, :], ones_row[:, :].unsqueeze(1).to_broadcast([MP, B * H, T]))\
                .then_inc(s["ones_in"], 16)
            act.wait_ge(s["warm_ready"], 1)
            nc.scalar.activation(warm_act[:], warm[:, 0:1], ACT.Exp)
            def qk_parts(b):
                act.wait_ge(s["xn_tr"], b + 1)
                copy(xn_t[:, b, :], bank(b)).then_inc(s["xn_t_ready"], 1)
                act.wait_ge(s["bias_in"], 32)
                for w in range(2):
                    n = 2 * b + w
                    act.wait_ge(s["qk_mm"], n + 1)
                    nc.scalar.activation(full[:, w, b, :], bank(2 + w), ACT.Identity,
                                         bias=b_qk_sb[:, w:w + 1]).then_inc(s["full_ready"], 1)
                    nc.scalar.activation(part[:, w, 0, b, :], bank(2 + w), ACT.Identity,
                                         bias=b_qk_sb[:, w:w + 1]).then_inc(s["hi_ready"], 1)
                for w in range(2):
                    act.wait_ge(s["rest_ready"], 2 * b + w + 1)
                    copy(part[:, w, 1, b, :], rest[:, w, b, :]).then_inc(s["mid_ready"], 1)

            qk_parts(0)
            act.wait_ge(s["kv_blk_zero"], 2)
            for w, (mm, read, blk) in enumerate((("kt_mm", "kt_read", k_blk), ("vt_mm", "vt_read", v_blk))):
                act.wait_ge(s[mm], 1)
                for half in range(2):
                    rows = slice(64 * half, 64 * half + 64)
                    last = copy(blk[rows, :, :, half, :],
                                ps[rows, 4 + w, :].rearrange("p (c b j) -> p c b j", c=XC, b=B))
                    last.then_inc(s[read], 1)
            qk_parts(1)
            for n in range(2):
                act.wait_ge(s["a_mm"], n + 1)
                copy(a_sb[:, :, n * 256:(n + 1) * 256].rearrange("p b (c j) -> p b c j", c=4),
                     ps[:, 6 + n, :].rearrange("p (c b j) -> p b c j", c=4, b=B)).then_inc(s["a_read"], 1)
            act.wait_ge(s["bm_mm"], 1)
            copy(bm_sb[:].rearrange("p b c d -> p (b c d)"),
                 ps[:, 4:6, :].rearrange("p a n -> p (a n)")).then_inc(s["bm_read"], 1)

            def o_copy(i):
                act.wait_ge(s["pv_done"], QT * (i + 1))
                if i >= 1:
                    act.wait_ge(s["o_tr"], i)
                copy(o_sb[:, :], bank(O_BANK)).then_inc(s["o_copied"], 1)

            def m_copy(i):
                act.wait_ge(s["m_tr"], i + 1)
                if i >= 1:
                    act.wait_ge(s["m_rows_even" if i % 2 else "m_rows_odd"], 16 * MP * ((i - 1) // 2 + 1))
                copy(m_t[:, :], bank(MISC)[0:MP * GH, 0:T // 2].bitcast(BF16)).then_inc(s["m_t_ready"], 1)

            def exps(i, kt):
                for pair in range(2):
                    u = KU * i + 2 * kt + pair
                    act.wait_ge(s["st_ready"], u + 1)
                    if i >= 1:
                        act.wait_ge(s["pv_done"], QT * (i - 1) + kt + 1)
                    bk = ST_BANK[pair]
                    nc.scalar.activation(probs[:, kt, 2 * pair:2 * pair + 2, kt * P:T],
                                         ps[:, bk:bk + 2, kt * P:T], ACT.Exp,
                                         scale=float(DH) ** -0.5).then_inc(s["exp_done"], 1)

            m_copy(0)
            for i in range(NG + 1):
                if i < NG:
                    exps(i, 0)
                if i >= 1:
                    o_copy(i - 1)
                if i + 1 < NG:
                    m_copy(i + 1)
                if i < NG:
                    for kt in range(1, QT):
                        exps(i, kt)

            def st_a(t):
                act.wait_ge(s["attn_tr"], t + 1)
                copy(tr_sb[:, 0, :], bank(0)[:, 0:P]).then_inc(s["attn_t_ready"], 1)

            def st_c(t):
                act.wait_ge(s["xn2_tr"], t + 1)
                copy(tr_sb[:, 1, :], bank(1)[:, 0:P]).then_inc(s["xn2_t_ready"], 1)

            def st_d(t):
                act.wait_ge(s["xsub_ready"], t + 1)
                nc.scalar.activation(xe[:, t % 2, :], xe[:, t % 2, :], ACT.Exp,
                                     scale=float(XD) ** -0.5).then_inc(s["xexp_done"], 1)

            def st_e(t):
                act.wait_ge(s["xp_tr"], t + 1)
                if t >= 2:
                    act.wait_ge(s["x2_mm"], t - 1)
                copy(xp_t[:, t % 2, :], bank(4)).then_inc(s["xp_t_ready"], 1)

            def st_f(t):
                act.wait_ge(s["xn3_tr"], t + 1)
                copy(tr_sb[:, 2, :], bank(0)[:, P:2 * P]).then_inc(s["xn3_t_ready"], 1)

            for step in range(NT + 5):
                for fn, lag in ((st_a, 0), (st_f, 5), (st_c, 1), (st_d, 2), (st_e, 3)):
                    if 0 <= step - lag < NT:
                        fn(step - lag)

            def mx_a(n):
                act.wait_ge(s["routed_tr"], n + 1)
                if n >= 2:
                    act.wait_ge(s["up_mm"], n - 1)
                copy(routed_t[:, n % 2, :], bank(0)[:, 0:P]).then_inc(s["routed_t_ready"], 1)

            def mx_b(n):
                act.wait_ge(s["gate_mm"], n + 1)
                if n >= 2:
                    act.wait_ge(s["hidden_ready"], n - 1)
                nc.scalar.activation(act_gate[:, n % 2, :], bank(1 + n % 2)[:, 0:I], ACT.Silu)\
                    .then_inc(s["silu_done"], 1)

            def mx_c(n):
                act.wait_ge(s["hidden_tr"], n + 1)
                if n >= 2:
                    act.wait_ge(s["y_mm"], n - 1)
                copy(hidden_t[:, n % 2, 0:2, :], bank(5)[:, 0:2 * P].rearrange("p (c q) -> p c q", c=2))
                copy(hidden_t[0:IR, n % 2, 2, :], bank(5)[0:IR, 2 * P:3 * P]).then_inc(s["hidden_t_ready"], 1)

            for step in range(NS + 2):
                for fn, lag in ((mx_a, 0), (mx_b, 1), (mx_c, 2)):
                    if 0 <= step - lag < NS:
                        fn(step - lag)

        @block.gpsimd
        def _(pool):
            nc.gpsimd.memset(warm[:], 0.0).then_inc(s["warm_ready"], 1)
            nc.gpsimd.memset(ones_row[:], 1.0).then_inc(s["ones_ready"], 1)
            nc.gpsimd.memset(neg_half[:], -0.5).then_inc(s["pool_chain"], 1)
            nc.gpsimd.memset(empty_row[:, 0:2 * D], 0.0).then_inc(s["zero_ready"], 1)
            nc.gpsimd.memset(empty_row[:, 2 * D:PW].bitcast(I32), 2 * NT * P).then_inc(s["zero_ready"], 1)
            pool.wait_ge(s["pool_chain"], 1)
            chain = [1]

            def link(ins):
                chain[0] += 1
                ins.then_inc(s["pool_chain"], 1)
                pool.wait_ge(s["pool_chain"], chain[0])

            def inv_std(ln, lo, hi, name):
                link(nc.gpsimd.tensor_scalar(var_eps[:, ln, lo:hi], mv[:, ln, lo:hi, 1], EPS, None, ALU.add))
                nc.gpsimd.tensor_tensor(rstd[:, ln, lo:hi], var_eps[:, ln, lo:hi], neg_half[:, lo:hi], ALU.pow)\
                    .then_inc(s[name], 1)

            for b in range(B):
                pool.wait_ge(s["ln1_stats"], QT * (b + 1))
                inv_std(0, b * QT, (b + 1) * QT, "rstd1")
            link(nc.gpsimd.memset(vg[:], 0.0))
            link(nc.gpsimd.memset(vg[:, :, :, DH:DH + 1], 1.0))
            nc.gpsimd.memset(k_blk[:], 0.0).then_inc(s["kv_blk_zero"], 1)
            nc.gpsimd.memset(v_blk[:], 0.0).then_inc(s["kv_blk_zero"], 1)
            pool.wait_ge(s["x0_in"], 16)
            pool.wait_ge(s["x1_in"], 16)
            pool.wait_ge(s["xbias_in"], 32)
            nc.gpsimd.tensor_tensor(xb[:], x_sb[:], b_proj_sb[:, :].unsqueeze(1).to_broadcast([P, NT, D]), ALU.add)\
                .then_inc(s["xb_ready"], 1)
            pool.wait_ge(s["v_ready"], B)
            for i in range(NG):
                for kt in range(QT):
                    if i >= 1:
                        pool.wait_ge(s["pv_done"], QT * (i - 1) + kt + 1)
                    nc.gpsimd.tensor_copy(vg[:, kt, :, 0:DH],
                                          v_sb[:, QT * (i // GPB) + kt, GH * (i % GPB):GH * (i % GPB) + GH, :])\
                        .then_inc(s["vg_ready"], 1)
                    for pair in range(2):
                        pool.wait_ge(s["exp_done"], KU * i + 2 * kt + pair + 1)
                        blk = probs[:, kt, 2 * pair:2 * pair + 2, kt * P:(kt + 1) * P]
                        nc.gpsimd.affine_select(out=blk, in_=blk, compare_op=ALU.is_ge, fill=0.0, base=0,
                                                pattern=[[0, 2], [1, P]], channel_multiplier=-1)\
                            .then_inc(s["masked"], 1)

            def st_b(t):
                pool.wait_ge(s["ln2_stats"], t + 1)
                inv_std(1, t, t + 1, "rstd2")

            def st_b2(t):
                nc.gpsimd.tensor_tensor(x1b[:, t, :], x1[:, t, :], bo_sb[:], ALU.add).then_inc(s["x1b_ready"], 1)

            def st_d(t):
                pool.wait_ge(s["xinv_ready"], t + 1)
                if t >= 2:
                    pool.wait_ge(s["xp_tr"], t - 1)
                nc.gpsimd.tensor_tensor(xp[:, t % 2, :].rearrange("p (h j) -> p h j", h=XH),
                                        xe[:, t % 2, :].rearrange("p (h j) -> p h j", h=XH),
                                        xs_sum[:, t % 2, :].unsqueeze(2).to_broadcast([P, XH, CT]), ALU.mult)\
                    .then_inc(s["xp_ready"], 1)

            def st_e(t):
                pool.wait_ge(s["ln3_stats"], t + 1)
                inv_std(2, t, t + 1, "rstd3")

            for step in range(NT + 4):
                for fn, lag in ((st_e, 4), (st_b, 0), (st_d, 2), (st_b2, 0)):
                    if 0 <= step - lag < NT:
                        fn(step - lag)
            pool.wait_ge(s["slot_ready"], 1)
            pool.wait_ge(s["zero_out"], 16 * NG)
            for t in range(NT):
                nc.gpsimd.indirect_dma_start(routed_dram, bass.IndirectOffsetOnAxis(ap=slot[:, t:t + 1], axis=0),
                                             row[:, t, :], None).then_inc(s["scattered"], 16)
            for n in range(NS):
                pool.wait_ge(s["y_ready"], n + 1)
                nc.gpsimd.indirect_dma_start(
                    out.rearrange("b t d -> (b t) d"),
                    bass.IndirectOffsetOnAxis(ap=routed[:, n, 2 * D:PW].bitcast(I32), axis=0),
                    y_sb[:, n % YB, :], None, bounds_check=NT * P - 1, oob_is_err=False)\
                    .then_inc(s[f"out_done{n % YB}"], 16)
            for k in range(YB):
                pool.wait_ge(s[f"out_done{k}"], 16 * len(range(k, NS, YB)))

        @block.vector
        def _(dve):
            chain = [0]

            def link(ins):
                chain[0] += 1
                ins.then_inc(s["dve_chain"], 1)
                dve.wait_ge(s["dve_chain"], chain[0])

            v = nc.vector

            def stats(ln, t, src, name):
                link(v.bn_stats(stat[:, ln, t, :], src))
                v.bn_aggr(mv[:, ln, t, :], stat[:, ln, t, :]).then_inc(s[name], 1)

            def normalise(dst, src, ln, t):
                return v.tensor_scalar(dst, src, mv[:, ln, t, 0:1], rstd[:, ln, t:t + 1], ALU.subtract, ALU.mult)

            for b in range(B):
                dve.wait_ge(s[f"x{b}_in"], 16)
                for t in range(b * QT, (b + 1) * QT):
                    v.bn_stats(stat[:, 0, t, :], x_sb[:, t, :]).then_inc(s["ln1_sums"], 1)
                for t in range(b * QT, (b + 1) * QT):
                    dve.wait_ge(s["ln1_sums"], t + 1)
                    v.bn_aggr(mv[:, 0, t, :], stat[:, 0, t, :]).then_inc(s["ln1_stats"], 1)
                if b == 0:
                    v.memset(ones_bf[:], 1.0)
                    v.memset(zeros_e[:], 0.0)
                    dve.wait_ge(s["const_in"], 16)
                    v.tensor_copy(cbf[:], cst[:, 0:3 * P]).then_inc(s["const_ready"], 1)
                    v.tensor_copy(row_token, token_number)
                dve.wait_ge(s["rstd1"], b + 1)
                dve.wait_ge(s["ln1_stats"], QT * (b + 1))
                for t in range(b * QT, (b + 1) * QT):
                    normalise(xn[:, t, :], x_sb[:, t, :], 0, t).then_inc(s["xn_ready"], 1)
            for b in range(B):
                for w in range(2):
                    n = 2 * b + w
                    dve.wait_ge(s["full_ready"], n + 1)
                    dve.wait_ge(s["hi_ready"], n + 1)
                    v.tensor_tensor(rest[:, w, b, :], full[:, w, b, :], part[:, w, 0, b, :], ALU.subtract)\
                        .then_inc(s["rest_ready"], 1)
                for w in range(2):
                    n = 2 * b + w
                    dve.wait_ge(s["mid_ready"], n + 1)
                    dve.wait_ge(s["rest_ready"], n + 1)
                    v.tensor_tensor(part[:, w, 2, b, :], rest[:, w, b, :], part[:, w, 1, b, :], ALU.subtract)\
                        .then_inc(s["low_ready"], 1)
                dve.wait_ge(s["v_mm"], b + 1)
                dve.wait_ge(s["bias_in"], 32)
                v.tensor_tensor(v_sb[:, b * QT:(b + 1) * QT, :, :].rearrange("p t h d -> p t (h d)"),
                                ps[:, 6 + b, :].rearrange("p (t n) -> p t n", t=QT),
                                b_v_sb[:, :].unsqueeze(1).to_broadcast([P, QT, D]), ALU.add)\
                    .then_inc(s["v_ready"], 1)

            def maxima(i, lo, hi):
                if lo == 0 and i >= 2:
                    dve.wait_ge(s["mparts_ready"], i - 1)
                for u in range(lo, hi):
                    qt, j, heads = units[u]
                    dve.wait_ge(s["unit_ready"], UNITS * i + u + 1)
                    w = (qt + 1) * P
                    v.tensor_reduce(mx[:, i % 2, qt, j:j + heads],
                                    bank(S_BANK[u % 2])[:, 0:heads * w].rearrange("p (h k) -> p h k", h=heads),
                                    AX.X, ALU.max).then_inc(s["unit_read"], 1)

            def max_parts(i):
                dve.wait_ge(s["unit_read"], UNITS * (i + 1))
                if i >= 1:
                    dve.wait_ge(s["m_tr"], i)
                hi, low = mparts[:, :, 0, :], mparts[:, :, 1, :]
                link(v.tensor_scalar(hi, mx[:, i % 2], -1.0, None, ALU.mult))
                v.scalar_tensor_tensor(out=low, in0=mx[:, i % 2], scalar=-1.0, in1=hi, op0=ALU.mult,
                                       op1=ALU.subtract).then_inc(s["mparts_ready"], 1)

            def attn_out(i):
                dve.wait_ge(s["o_tr"], i + 1)
                o = bank(MISC).rearrange("p (t h w) -> p t h w", t=QT, h=GH)
                link(v.reciprocal(den[:], o[:, :, :, DH]))
                b, g = i // GPB, i % GPB
                v.tensor_tensor(attn[:, b * QT:(b + 1) * QT, GH * g:GH * (g + 1), :], o[:, :, :, 0:DH],
                                den[:].unsqueeze(3).to_broadcast([P, QT, GH, DH]), ALU.mult)\
                    .then_inc(s["attn_ready"], 1)

            for i in range(2):
                maxima(i, 0, UNITS)
                max_parts(i)
            for i in range(NG + 1):
                if i + 2 < NG:
                    maxima(i + 2, 0, 6)
                if i >= 1:
                    attn_out(i - 1)
                if i + 2 < NG:
                    maxima(i + 2, 6, UNITS)
                    max_parts(i + 2)

            def heads(ap):
                return ap.rearrange("p (h j) -> p h j", h=XH)

            def over_keys(ap):
                return ap.unsqueeze(2).to_broadcast([P, XH, CT])

            def x1_add(t):
                dve.wait_ge(s["x1_mm"], t + 1)
                if t == 0:
                    dve.wait_ge(s["xb_ready"], 1)
                v.tensor_tensor(x1[:, t, :], bank(2)[:, 0:P], xb[:, t, :], ALU.add).then_inc(s["x1_ready"], 1)

            def ln2_sums(t):
                dve.wait_ge(s["x1_ready"], t + 1)
                v.bn_stats(stat[:, 1, t, :], x1[:, t, :]).then_inc(s["ln2_sums"], 1)

            def ln2_stats(t):
                dve.wait_ge(s["ln2_sums"], t + 1)
                v.bn_aggr(mv[:, 1, t, :], stat[:, 1, t, :]).then_inc(s["ln2_stats"], 1)

            def norm2(t):
                dve.wait_ge(s["rstd2"], t + 1)
                dve.wait_ge(s["ln2_stats"], t + 1)
                if t >= 2:
                    dve.wait_ge(s["xn2_tr"], t - 1)
                normalise(xn2[:, t % 2, :], x1[:, t, :], 1, t).then_inc(s["xn2_ready"], 1)

            def xmax(t):
                dve.wait_ge(s["xs_mm"], t + 1)
                v.tensor_reduce(xm[:, t % 2, :], heads(bank(6 + t % 2)), AX.X, ALU.max).then_inc(s["xmax_ready"], 1)

            def xsub(t):
                dve.wait_ge(s["xmax_ready"], t + 1)
                if t >= 2:
                    dve.wait_ge(s["xp_ready"], t - 1)
                v.tensor_tensor(heads(xe[:, t % 2, :]), heads(bank(6 + t % 2)), over_keys(xm[:, t % 2, :]),
                                ALU.subtract).then_inc(s["xsub_ready"], 1)

            def xsum(t):
                dve.wait_ge(s["xexp_done"], t + 1)
                v.tensor_reduce(xs_sum[:, t % 2, :], heads(xe[:, t % 2, :]), AX.X, ALU.add).then_inc(s["xsum_ready"], 1)

            def xinv(t):
                dve.wait_ge(s["xsum_ready"], t + 1)
                v.reciprocal(xs_sum[:, t % 2, :], xs_sum[:, t % 2, :]).then_inc(s["xinv_ready"], 1)

            def x2_add(t):
                dve.wait_ge(s["x2_mm"], t + 1)
                dve.wait_ge(s["x1b_ready"], t + 1)
                v.tensor_tensor(x2[:, t, :], bank(3)[:, 0:P], x1b[:, t, :], ALU.add).then_inc(s["x2_ready"], 1)

            def ln3_sums(t):
                dve.wait_ge(s["x2_ready"], t + 1)
                v.bn_stats(stat[:, 2, t, :], x2[:, t, :]).then_inc(s["ln3_sums"], 1)

            def ln3_stats(t):
                dve.wait_ge(s["ln3_sums"], t + 1)
                v.bn_aggr(mv[:, 2, t, :], stat[:, 2, t, :]).then_inc(s["ln3_stats"], 1)

            def norm3(t):
                dve.wait_ge(s["rstd3"], t + 1)
                dve.wait_ge(s["ln3_stats"], t + 1)
                normalise(xn3[:, t, :], x2[:, t, :], 2, t).then_inc(s["xn3_ready"], 1)

            for step in range(NT + 4):
                for fn, lag in ((xmax, 2), (x2_add, 4), (norm2, 1), (ln3_sums, 4), (xsub, 2), (x1_add, 0),
                                (ln3_stats, 4), (ln2_sums, 0), (xsum, 2), (ln2_stats, 0), (norm3, 4), (xinv, 2)):
                    if 0 <= step - lag < NT:
                        fn(step - lag)

            dve.wait_ge(s["logits_mm"], NT)
            lg = bank(5)[:, 0:NT * E].rearrange("p (t e) -> p t e", t=NT)

            def over_e(ap):
                return ap.unsqueeze(2).to_broadcast([P, NT, E])

            def over_t(ap):
                return ap.unsqueeze(1).to_broadcast([P, NT, E])

            link(v.tensor_reduce(logit_max[:], lg, AX.X, ALU.max))
            link(v.tensor_tensor(first[:], lg, over_e(logit_max[:]), ALU.is_equal))
            link(v.tensor_tensor(first[:], first[:], over_t(first_rank), ALU.mult))
            link(v.tensor_reduce(first_max[:], first[:], AX.X, ALU.max))
            link(v.tensor_tensor(chosen[:], first[:], over_e(first_max[:]), ALU.is_equal))
            v.tensor_copy(chosen_bf[:], chosen[:]).then_inc(s["chosen_ready"], 1)
            dve.wait_ge(s["counts_mm"], 1)
            cnt = bank(6)[:, 0:E]
            link(v.tensor_tensor(over[:], cnt.unsqueeze(2).to_broadcast([P, E, NT]), tile_edges, ALU.is_gt))
            link(v.tensor_reduce(expert_tiles[:], over[:], AX.X, ALU.add))
            link(v.tensor_tensor_scan(tiles_end[:], expert_tiles[:], zeros_e[:], 0.0, ALU.add, ALU.add))
            link(v.tensor_tensor(run_start[:], tiles_end[:], expert_tiles[:], ALU.subtract))
            link(v.tensor_scalar(run_start[:], run_start[:], float(P), None, ALU.mult))
            rank = bank(7)[:, 0:NT * E].rearrange("p (t e) -> p t e", t=NT)
            link(v.tensor_tensor(slot_e[:], rank, over_t(run_start[:]), ALU.add))
            link(v.tensor_tensor(slot_e[:], slot_e[:], chosen[:], ALU.mult))
            link(v.tensor_reduce(slot_f[:], slot_e[:], AX.X, ALU.add))
            dve.wait_ge(s["xn3_ready"], NT)
            v.tensor_copy(slot[:], slot_f[:]).then_inc(s["slot_ready"], 1)
            link(v.tensor_tensor(past[:], tiles_end[:].unsqueeze(1).to_broadcast([P, NS, E]), tile_index, ALU.is_le))
            link(v.tensor_reduce(tile_expert_f[:, 0, :], past[:], AX.X, ALU.add))
            link(v.tensor_scalar(tile_expert_f[:, 1, :], tile_expert_f[:, 0, :], float(E - 1), float(IC * D),
                                 ALU.min, ALU.mult))
            link(v.tensor_scalar(tile_expert_f[:, 0, :], tile_expert_f[:, 0, :], float(E - 1), float(2 * I),
                                 ALU.min, ALU.mult))
            v.tensor_copy(tile_expert[:], tile_expert_f[:]).then_inc(s["experts_known"], 1)

            def mx_b(n):
                dve.wait_ge(s["silu_done"], n + 1)
                dve.wait_ge(s["up_mm"], n + 1)
                if n >= 2:
                    dve.wait_ge(s["hidden_tr"], n - 1)
                v.tensor_tensor(hidden[:, n % 2, :], bank(3 + n % 2)[:, 0:I], act_gate[:, n % 2, :], ALU.mult)\
                    .then_inc(s["hidden_ready"], 1)

            def mx_d(n):
                dve.wait_ge(s["y_mm"], n + 1)
                for c, (n0, _) in enumerate(READS):
                    if n == n0:
                        dve.wait_ge(s[f"routed_in{c}"], 16)
                if n >= YB:
                    dve.wait_ge(s[f"out_done{n % YB}"], 16 * (n // YB))
                v.tensor_tensor(y_sb[:, n % YB, :], bank(6 + n % 2)[:, 0:D], routed[:, n, D:2 * D], ALU.add)\
                    .then_inc(s["y_ready"], 1)

            for step in range(NS + 3):
                for fn, lag in ((mx_b, 1), (mx_d, 3)):
                    if 0 <= step - lag < NS:
                        fn(step - lag)

        @block.tensor
        def _(pe):
            def mm(o, lhs, rhs, start=True, stop=True):
                return nc.tensor.matmul(o, lhs, rhs, start=start, stop=stop)

            pe.wait_ge(s["warm_ready"], 1)
            for _ in range(WARM):
                mm(bank(7), warm[:, 0:P], warm[:])
            pe.wait_ge(s["const_in"], 16)

            def qkv(b):
                for t in range(QT):
                    n = b * QT + t
                    pe.wait_ge(s["xn_ready"], n + 1)
                    last = nc.tensor.transpose(bank(b)[:, t * P:(t + 1) * P], xn[:, n, :], ident)
                last.then_inc(s["xn_tr"], 1)
                pe.wait_ge(s["w_attn_in"], 16)
                pe.wait_ge(s["xn_t_ready"], b + 1)
                for w in range(2):
                    if b >= 1:
                        pe.wait_ge(s["hi_ready"], w + 1)
                    mm(bank(2 + w), w_attn_sb[:, w * D:(w + 1) * D], xn_t[:, b, :]).then_inc(s["qk_mm"], 1)
                for t in range(QT):
                    last = mm(bank(6 + b)[:, t * D:(t + 1) * D], xn_t[:, b, t * P:(t + 1) * P],
                              w_attn_sb[:, 2 * D:3 * D])
                last.then_inc(s["v_mm"], 1)

            qkv(0)
            pe.wait_ge(s["ctx_in"], 16)
            pe.wait_ge(s["wkv_in"], 32)
            for w, (name, wt) in enumerate((("kt_mm", wk_sb), ("vt_mm", wv_sb))):
                for c in range(XC):
                    last = mm(bank(4 + w)[:, c * B * CT:(c + 1) * B * CT], wt[:, c * P:(c + 1) * P], ctx_sb[:])
                last.then_inc(s[name], 1)
            qkv(1)
            pe.wait_ge(s["wqo_in"], 32)
            pe.wait_ge(s["kt_read"], 2)
            pe.wait_ge(s["v_ready"], B)
            for c in range(XC):
                last = mm(bank(6 + c // 4)[:, (c % 4) * P:(c % 4 + 1) * P], wq_sb[:, c, :],
                          k_blk[:, c].rearrange("p b h j -> p (b h j)"))
                if c % 4 == 3:
                    last.then_inc(s["a_mm"], 1)
            pe.wait_ge(s["vt_read"], 2)
            for b in range(B):
                for c in range(XC):
                    rows = slice(64 * (c % 2), 64 * (c % 2) + 64)
                    last = mm(ps[rows, 4 + b, (c // 2) * D:(c // 2 + 1) * D],
                              v_blk[:, c, b].rearrange("p h j -> p (h j)"), wo_sb[:, c, :])
            last.then_inc(s["bm_mm"], 1)

            def scores(i, lo, hi):
                for u in range(lo, hi):
                    qt, j0, heads = units[u]
                    w = (qt + 1) * P
                    n = UNITS * i + u
                    if n >= 2:
                        pe.wait_ge(s["unit_read"], n - 1)
                    for j in range(heads):
                        hh = GH * i + j0 + j
                        o = bank(S_BANK[u % 2])[:, j * w:(j + 1) * w]
                        mm(o, qs[0:SC, hh, qt * P:(qt + 1) * P], ks[0:SC, hh, 0:w], stop=False)
                        last = mm(o[:, qt * P:w], ident_bf, causal_bf, start=False)
                    last.then_inc(s["unit_ready"], 1)

            def max_transposes(i):
                pe.wait_ge(s["mparts_ready"], i + 1)
                if i >= 3:
                    pe.wait_ge(s["attn_ready"], i - 2)
                for qt in range(QT):
                    last = nc.tensor.transpose(bank(MISC)[0:MP * GH, qt * P // 2:(qt + 1) * P // 2].bitcast(BF16),
                                               mparts[:, qt].rearrange("p c h -> p (c h)"), ident_bf)
                last.then_inc(s["m_tr"], 1)

            def scores_t(i, kt, pair):
                if kt == 0 and pair == 0:
                    pe.wait_ge(s["m_rows_odd" if i % 2 else "m_rows_even"], 16 * MP * (i // 2 + 1))
                u = KU * i + 2 * kt + pair
                if u >= 2:
                    pe.wait_ge(s["exp_done"], u - 1)
                for j in range(2):
                    hh = GH * i + 2 * pair + j
                    last = mm(bank(ST_BANK[pair] + j)[:, kt * P:T], ks[0:SA, hh, kt * P:(kt + 1) * P],
                              qs[0:SA, hh, kt * P:T])
                last.then_inc(s["st_ready"], 1)

            def weighted(i, kt):
                pe.wait_ge(s["masked"], KU * i + 2 * kt + 2)
                pe.wait_ge(s["vg_ready"], QT * i + kt + 1)
                if kt == 0 and i >= 1:
                    pe.wait_ge(s["o_copied"], i)
                for j in range(GH):
                    last = mm(ps[VW * j:VW * (j + 1), O_BANK, kt * P:T], vg[:, kt, j, :], probs[:, kt, j, kt * P:T],
                              start=(kt == 0), stop=(kt == QT - 1))
                last.then_inc(s["pv_done"], 1)

            def o_transposes(i):
                pe.wait_ge(s["o_copied"], i + 1)
                pe.wait_ge(s["m_t_ready"], min(i + 3, NG))
                if i >= 1:
                    pe.wait_ge(s["attn_ready"], i)
                for qt in range(QT):
                    last = nc.tensor.transpose(bank(MISC)[:, qt * P:(qt + 1) * P], o_sb[:, qt * P:(qt + 1) * P], ident)
                last.then_inc(s["o_tr"], 1)

            pe.wait_ge(s["const_ready"], 1)
            pe.wait_ge(s["v_ready"], B)
            pe.wait_ge(s["stack0_first"], 16 * 6)
            pe.wait_ge(s["a_read"], 2)
            scores(0, 0, UNITS)
            max_transposes(0)
            pe.wait_ge(s["stack0_in"], 16 * 6)
            scores(1, 0, UNITS)
            pe.wait_ge(s["ones_in"], 16)
            pe.wait_ge(s["bm_read"], 1)
            for i in range(NG + 1):
                if i + 2 == GPB:
                    pe.wait_ge(s["stack1_first"], 16 * 6)
                    pe.wait_ge(s["stack1_in"], 16 * 6)
                for kt in range(QT):
                    if i < NG:
                        scores_t(i, kt, 0)
                    if i + 2 < NG:
                        scores(i + 2, 3 * kt, 3 * kt + 1)
                    if i < NG:
                        scores_t(i, kt, 1)
                    if i + 2 < NG:
                        scores(i + 2, 3 * kt + 1, 3 * kt + 2)
                    if kt >= 1 and i < NG:
                        weighted(i, kt - 1)
                    if kt == 0 and i >= 1:
                        weighted(i - 1, QT - 1)
                    if kt == 0 and i + 1 < NG:
                        max_transposes(i + 1)
                    if kt == 1 and i >= 1:
                        o_transposes(i - 1)
                    if i + 2 < NG:
                        scores(i + 2, 3 * kt + 2, 3 * kt + 3)

            pe.wait_ge(s["proj_in"], 16)

            def st_a(t):
                if t == 0:
                    pe.wait_ge(s["attn_ready"], NG)
                if t >= 6:
                    pe.wait_ge(s["xn3_t_ready"], t - 5)
                nc.tensor.transpose(bank(0)[:, 0:P], attn[:, t].rearrange("p h d -> p (h d)"), ident)\
                    .then_inc(s["attn_tr"], 1)

            def st_a2(t):
                pe.wait_ge(s["attn_t_ready"], t + 1)
                if t >= 1:
                    pe.wait_ge(s["x1_ready"], t)
                mm(bank(2)[:, 0:D], tr_sb[:, 0, :], w_proj_sb[:]).then_inc(s["x1_mm"], 1)

            def st_c(t):
                pe.wait_ge(s["xn2_ready"], t + 1)
                if t >= 1:
                    pe.wait_ge(s["xn2_t_ready"], t)
                nc.tensor.transpose(bank(1)[:, 0:P], xn2[:, t % 2, :], ident).then_inc(s["xn2_tr"], 1)

            def st_c2(t):
                pe.wait_ge(s["xn2_t_ready"], t + 1)
                if t >= 2:
                    pe.wait_ge(s["xsub_ready"], t - 1)
                mm(bank(6 + t % 2), tr_sb[:, 1, :], a_sb[:, t // QT, :]).then_inc(s["xs_mm"], 1)

            def st_e(t):
                pe.wait_ge(s["xp_ready"], t + 1)
                if t >= 1:
                    pe.wait_ge(s["xp_t_ready"], t)
                for c in range(4):
                    last = nc.tensor.transpose(bank(4)[:, c * P:(c + 1) * P], xp[:, t % 2, c * P:(c + 1) * P], ident)
                last.then_inc(s["xp_tr"], 1)

            def st_e2(t):
                pe.wait_ge(s["xp_t_ready"], t + 1)
                if t >= 1:
                    pe.wait_ge(s["x2_ready"], t)
                for c in range(4):
                    last = mm(bank(3)[:, 0:D], xp_t[:, t % 2, c * P:(c + 1) * P], bm_sb[:, t // QT, c, :],
                              start=(c == 0), stop=(c == 3))
                last.then_inc(s["x2_mm"], 1)

            def st_f(t):
                pe.wait_ge(s["xn3_ready"], t + 1)
                pe.wait_ge(s["attn_t_ready"], min(t + 6, NT))
                if t >= 1:
                    pe.wait_ge(s["xn3_t_ready"], t)
                nc.tensor.transpose(bank(0)[:, P:2 * P], xn3[:, t, :], ident).then_inc(s["xn3_tr"], 1)

            def st_f2(t):
                pe.wait_ge(s["xn3_t_ready"], t + 1)
                if t == 0:
                    pe.wait_ge(s["router_in"], 16)
                mm(bank(5)[:, t * E:(t + 1) * E], tr_sb[:, 2, :], router_sb[:]).then_inc(s["logits_mm"], 1)

            for step in range(NT + 5):
                for fn, lag in ((st_a, 0), (st_f, 5), (st_a2, 0), (st_c, 1), (st_f2, 5), (st_e, 3),
                                (st_c2, 1), (st_e2, 3)):
                    if 0 <= step - lag < NT:
                        fn(step - lag)

            pe.wait_ge(s["chosen_ready"], 1)
            pe.wait_ge(s["xsub_ready"], NT)
            for t in range(NT):
                last = mm(bank(6)[:, 0:E], ones_bf[:], chosen_bf[:, t, :], start=(t == 0), stop=(t == NT - 1))
            mm(bank(7)[:, 0:NT * E], before_bf, chosen_bf[:].rearrange("p t e -> p (t e)"), stop=False)
            for back in range(1, NT):
                last = mm(bank(7)[:, back * E:NT * E], ones_bf[:],
                          chosen_bf[:, 0:NT - back].rearrange("p t e -> p (t e)"), start=False, stop=(back == NT - 1))
            last.then_inc(s["counts_mm"], 1)

            pe.wait_ge(s["experts_in"], 32)
            pe.wait_ge(s["experts_known"], 1)

            def mx_a(n):
                for c, (n0, _) in enumerate(READS):
                    if n == n0:
                        pe.wait_ge(s[f"routed_in{c}"], 16)
                if n >= 1:
                    pe.wait_ge(s["routed_t_ready"], n)
                nc.tensor.transpose(bank(0)[:, 0:P], routed[:, n, 0:D], ident).then_inc(s["routed_tr"], 1)

            def mx_b(n):
                off = pe.value_load(tile_expert[0:1, 0, n:n + 1], min_val=0, max_val=(E - 1) * 2 * I)
                pe.wait_ge(s["routed_t_ready"], n + 1)
                if n >= 2:
                    pe.wait_ge(s["silu_done"], n - 1)
                mm(bank(1 + n % 2)[:, 0:I], routed_t[:, n % 2, :], gate_up_sb[:, bass.ds(off, I)])\
                    .then_inc(s["gate_mm"], 1)
                if n >= 2:
                    pe.wait_ge(s["hidden_ready"], n - 1)
                mm(bank(3 + n % 2)[:, 0:I], routed_t[:, n % 2, :], gate_up_sb[:, bass.ds(off + I, I)])\
                    .then_inc(s["up_mm"], 1)

            def mx_c(n):
                pe.wait_ge(s["hidden_ready"], n + 1)
                if n >= 1:
                    pe.wait_ge(s["hidden_t_ready"], n)
                nc.tensor.transpose(bank(5)[:, 0:P], hidden[:, n % 2, 0:P], ident)
                nc.tensor.transpose(bank(5)[:, P:2 * P], hidden[:, n % 2, P:2 * P], ident)
                nc.tensor.transpose(bank(5)[0:IR, 2 * P:3 * P], hidden[:, n % 2, 2 * P:I], ident)\
                    .then_inc(s["hidden_tr"], 1)

            def mx_d(n):
                off = pe.value_load(tile_expert[0:1, 1, n:n + 1], min_val=0, max_val=(E - 1) * IC * D)
                pe.wait_ge(s["hidden_t_ready"], n + 1)
                if n >= 2:
                    pe.wait_ge(s["y_ready"], n - 1)
                o = bank(6 + n % 2)[:, 0:D]
                mm(o, hidden_t[:, n % 2, 0, :], down_sb[:, bass.ds(off, D)], stop=False)
                mm(o, hidden_t[:, n % 2, 1, :], down_sb[:, bass.ds(off + D, D)], start=False, stop=False)
                mm(o, hidden_t[0:IR, n % 2, 2, :], down_sb[0:IR, bass.ds(off + 2 * D, D)], start=False)\
                    .then_inc(s["y_mm"], 1)

            for step in range(NS + 3):
                for fn, lag in ((mx_a, 0), (mx_b, 1), (mx_c, 2), (mx_d, 3)):
                    if 0 <= step - lag < NS:
                        fn(step - lag)


def kernel(**inputs):
    import numpy as _np
    import concourse.bacc as _bacc
    from concourse import mybir as _mybir
    from concourse.bass_utils import run_bass_kernel_spmd as _run

    a = {k: _np.asarray(v) for k, v in inputs.items()}
    consts = _np.zeros((P, CONST_W), _np.float32)
    r = _np.arange(P)
    consts[:, 0:P] = r[:, None] == r[None, :]
    consts[:, P:2 * P] = _np.where(r[None, :] <= r[:, None], 0.0, -1e30)
    consts[:, 2 * P:3 * P] = r[:, None] < r[None, :]
    o0 = 3 * P
    consts[:, o0:o0 + E * NT] = _np.tile(P * _np.arange(NT), E)
    o0 += E * NT
    consts[:, o0:o0 + NS * E] = _np.repeat(_np.arange(NS), E)
    consts[:, o0 + NS * E:o0 + NS * E + E] = E - _np.arange(E)
    consts[:, CONST_W - NT:] = P * _np.arange(NT)[None, :] + r[:, None]
    down = a["L0_ffn_down_w"].transpose(0, 2, 1)
    down = _np.concatenate([down, _np.zeros((E, IC * P - I, D), down.dtype)], axis=1)
    b_attn = a["L0_attn_b_attn"]
    arrays = {
        "x": a["x"],
        "ctx_t": a["ctx_768"].transpose(2, 0, 1).reshape(CW, B * CT),
        "w_attn": a["L0_attn_W_attn"],
        "b_attn_qk": b_attn[0:2 * D].reshape(2, D).T,
        "b_attn_v": b_attn[2 * D:3 * D],
        "w_proj": a["L0_attn_W_proj"],
        "b_proj": a["L0_attn_b_proj"],
        "wq_t": a["L0_xattn_Wq"].T,
        "wk": a["L0_xattn_Wk"],
        "wv": a["L0_xattn_Wv"],
        "wo": a["L0_xattn_Wo"],
        "bo": a["L0_xattn_bo"],
        "router_t": a["L0_ffn_router_w"].T,
        "gate_up": _np.stack([a["L0_ffn_gate_w"], a["L0_ffn_up_w"]], axis=1)
                      .transpose(3, 0, 1, 2).reshape(D, E * 2 * I),
        "down": down.reshape(E, IC, P, D).transpose(2, 0, 1, 3).reshape(P, E * IC * D),
        "consts": consts,
    }
    nc = _bacc.Bacc("TRN2", target_bir_lowering=False, num_devices=1)
    feed, args = {}, {}
    for name, v in arrays.items():
        v = _np.ascontiguousarray(v)
        feed[f"in_{name}"] = v
        args[name] = nc.dram_tensor(f"in_{name}", v.shape, _mybir.dt.from_np(v.dtype), kind="ExternalInput").ap()
    out = nc.dram_tensor("out_0", (B, T, D), F32, kind="ExternalOutput").ap()
    decoder_layer(nc, out=out, **args)
    got = _run(nc, [feed], core_ids=[0])
    return got.results[0]["out_0"]
```

```python
from contextlib import ExitStack

import concourse.bass as bass
from concourse import mybir

F32 = mybir.dt.float32
BF16 = mybir.dt.bfloat16
I32 = mybir.dt.int32
ALU = mybir.AluOpType
ACT = mybir.ActivationFunctionType
AX = mybir.AxisListType

P = 128
B, T, D = 2, 512, 128
QT = T // P
NT = B * QT
H, DH = 16, 8
GH = 4
NG = B * H // GH
GPB = H // GH
SC = 9 * DH
MP = 2
SA = SC + MP
VW = 32
CT, CW = 32, 96
XH, XD = 16, 64
XC = XH * XD // P
XS = XH * CT
E, I = 8, 352
IC = 3
IR = I - 2 * P
PW = 2 * D + 1
RR = 32
STRIPS = P // RR
NU = (NT * P + E * (RR - 1)) // RR
NS = -(-NU // STRIPS)
READS = ((0, 1), (1, 3), (3, 6), (6, NS))
FILLS = 5
WARM_AGAIN = 3
WARM_LATER = 11
WARM = 12
YB = 4
EPS = 1e-5
LN3_LAG = 4
TA = 5
ROUND = float(1 << 23)
UNITS = 12
KU = 2 * QT
CONST_W = 3 * P + NS * STRIPS + E + NT



def max_units():
    units = []
    for qt in reversed(range(QT)):
        heads = {3: 1, 2: 1, 1: 2, 0: 2}[qt]
        units += [(qt, j, heads) for j in range(0, GH, heads)]
    return units


def decoder_layer(nc, x, ctx_t, w_attn, b_attn_qk, b_attn_v, w_proj, b_proj, wq_t, wk, wv, wo, bo,
                  router_t, gate_up, down, consts, out):
    units = max_units()
    assert len(units) == UNITS

    with ExitStack() as ctx:
        def sb(name, shape, dt=F32):
            return ctx.enter_context(nc.sbuf_tensor(name, shape, dt))

        def sem(name):
            return ctx.enter_context(nc.semaphore(name))

        q_parts_dram = nc.dram_tensor("q_parts_dram", (B, 3, DH, H, T), BF16, kind="Internal").ap()
        k_parts_dram = nc.dram_tensor("k_parts_dram", (B, 5, DH, H, T), BF16, kind="Internal").ap()
        routed_dram = nc.dram_tensor("routed_dram", (NS * P, PW), F32, kind="Internal").ap()

        cst = sb("cst", [P, CONST_W])
        ident = cst[:, 0:P]
        o0 = 3 * P
        unit_index = cst[:, o0:o0 + NS * STRIPS]
        o0 += NS * STRIPS
        first_rank = cst[:, o0:o0 + E]
        token_number = cst[:, CONST_W - NT:CONST_W]
        cbf = sb("cbf", [P, 3 * P], BF16)
        ident_bf, causal_bf, before_bf = cbf[:, 0:P], cbf[:, P:2 * P], cbf[:, 2 * P:3 * P]
        ones_bf = sb("ones_bf", [P, P], BF16)
        unit_share = sb("unit_share", [P, P], BF16)
        ones_row = sb("ones_row", [MP, T], BF16)
        neg_half = sb("neg_half", [P, NT])
        w_attn_sb = sb("w_attn_sb", [P, 3 * D])
        b_qk_sb = sb("b_qk_sb", [P, 2])
        b_v_sb = sb("b_v_sb", [P, D])
        w_proj_sb = sb("w_proj_sb", [P, D])
        b_proj_sb = sb("b_proj_sb", [P, D])
        bo_sb = sb("bo_sb", [P, D])
        ctx_sb = sb("ctx_sb", [CW, B * CT])
        router_sb = sb("router_sb", [P, E])

        x_sb = sb("x_sb", [P, NT, D])
        xb = sb("xb", [P, NT, D])
        xn = sb("xn", [P, NT, D])
        xn_t = sb("xn_t", [P, B, T])
        stat = sb("stat", [P, 3, NT, 6])
        mv = sb("mv", [P, 3, NT, 2])
        var_eps = sb("var_eps", [P, 2, NT])
        rstd = sb("rstd", [P, 2, NT])
        var3, neg_mean, rstd3, shift3 = (sb(name, [P, NT]) for name in ("var3", "neg_mean", "rstd3", "shift3"))
        part = sb("part", [P, 2, 3, B, T], BF16)
        qs = sb("qs", [P, B * H, T], BF16)
        ks = sb("ks", [P, B * H, T], BF16)
        gate_up_sb = qs[:].rearrange("p h t -> p (h t)").bitcast(F32)[:, 0:E * 2 * I]
        down_sb = ks[:].rearrange("p h t -> p (h t)").bitcast(F32)[:, 0:E * IC * D]
        n = E * 2 * I
        down_unit = qs[:].rearrange("p h t -> p (h t)").bitcast(F32)[:, n:n + 2 * (STRIPS - 1) * IC * D]\
            .rearrange("p (n j w) -> p n j w", n=2, j=STRIPS - 1)
        n = E * IC * D
        gate_up_unit = ks[:].rearrange("p h t -> p (h t)").bitcast(F32)[:, n:n + 2 * (STRIPS - 1) * 2 * I]\
            .rearrange("p (n j w) -> p n j w", n=2, j=STRIPS - 1)
        v_sb = sb("v_sb", [P, NT, H, DH])
        vg = sb("vg", [P, QT, GH, VW])
        mx = sb("mx", [P, 2, QT, GH])
        mparts = sb("mparts", [P, QT, MP, GH], BF16)
        m_t = sb("m_t", [MP * GH, T], BF16)
        probs = sb("probs", [P, QT, GH, T])
        room = probs[:].rearrange("p a h t -> p (a h t)")
        full = room[:, 0:2 * B * T].rearrange("p (w b t) -> p w b t", w=2, b=B)
        rest = room[:, 2 * B * T:4 * B * T].rearrange("p (w b t) -> p w b t", w=2, b=B)
        o0, n = 4 * B * T, XH * XD
        wk_sb = room[0:CW, o0:o0 + n]
        wv_sb = room[0:CW, o0 + n:o0 + 2 * n]
        wq_sb = room[:, o0 + 2 * n:o0 + 3 * n].rearrange("p (c d) -> p c d", c=XC)
        wo_sb = room[:, o0 + 3 * n:o0 + 4 * n].rearrange("p (c d) -> p c d", c=XC)
        routed = room[:, 0:NS * PW].rearrange("p (n w) -> p n w", n=NS)
        o0 = NS * PW
        y_sb = room[:, o0:o0 + YB * D].rearrange("p (n d) -> p n d", n=YB)
        o0 += YB * D
        hidden_t = room[:, o0:o0 + 2 * IC * P].rearrange("p (n c q) -> p n c q", n=2, c=IC)
        o_sb = sb("o_sb", [P, T])
        attn = sb("attn", [P, NT, H, DH])
        den = sb("den", [P, QT, GH])
        k_blk = sb("k_blk", [P, XC, B, 2, CT])
        v_blk = sb("v_blk", [P, XC, B, 2, CT])
        a_sb = sb("a_sb", [P, B, XS])
        bm_sb = sb("bm_sb", [P, B, 4, D])
        attn_t = xn[:, 0:QT, :].rearrange("p t d -> p (t d)")
        xn2 = xn[:, QT:NT, :]
        xn2_t = xn_t
        xn3_t = sb("xn3_t", [P, P])
        x1 = sb("x1", [P, NT, D])
        xm = sb("xm", [P, 2, XH])
        xe = sb("xe", [P, 2, XS])
        xp = sb("xp", [P, 2, XS])
        xs_sum = sb("xs_sum", [P, 2, XH])
        xp_t = sb("xp_t", [P, 2, XS])
        row = sb("row", [P, NT, PW])
        xn3, x2 = row[:, :, 0:D], row[:, :, D:2 * D]
        row_token = row[:, :, 2 * D].bitcast(I32)
        logit_max = sb("logit_max", [P, NT])
        first = sb("first", [P, NT, E])
        first_max = sb("first_max", [P, NT])
        chosen_bf = sb("chosen_bf", [P, NT, E], BF16)
        units_so_far = sb("units_so_far", [P, 2, E])
        units_new = sb("units_new", [P, 2, E])
        units_end = sb("units_end", [P, 1 + 2 * E])
        zeros_e = sb("zeros_e", [P, E])
        old_end = sb("old_end", [P, E])
        shift = sb("shift", [P, E])
        beyond = sb("beyond", [P, NT - TA, E])
        slot_e = sb("slot_e", [P, NT, E])
        slot_f = sb("slot_f", [P, NT])
        slot = sb("slot", [P, NT], I32)
        past = sb("past", [P, NS * STRIPS, 2 * E])
        in_second = sb("in_second", [P, NS * STRIPS])
        ends_past = sb("ends_past", [P, NS * STRIPS])
        unit_expert = sb("unit_expert", [P, 2, NS * STRIPS], I32)
        empty_row = sb("empty_row", [P, PW])
        routed_t = sb("routed_t", [P, 2, P])
        act_gate = sb("act_gate", [P, 2, I])
        hidden = sb("hidden", [P, 2, I])

        warm = sb("warm", [P, T], BF16)
        warm_act = sb("warm_act", [P, 1])

        ps = ctx.enter_context(nc.psum_tensor("ps", [P, 8, T], F32))

        names = """x0_in x1_in warm_ready ln1_sums w_attn_in bias_in const_in ctx_in wkv_in wqo_in proj_in xbias_in
            router_in experts_in const_ready ones_ready dve_chain pool_chain ln1_stats rstd1
            xn_ready xn_tr xn_t_ready qk_mm v_mm v_ready full_ready hi_ready rest_ready mid_ready
            low_ready parts_out0 parts_out1 stack0_first stack0_in stack1_first stack1_in ones_in
            kt_mm kt_read vt_mm vt_read kv_blk_zero a_mm a_read bm_mm bm_read unit_ready unit_read
            mparts_ready m_tr m_t_ready m_rows_even m_rows_odd st_ready exp_done masked pv_done
            o_copied o_tr attn_ready attn_tr attn_t_ready x1_mm x1_ready ln2_stats xn2_ready xn2_tr
            xn2_t_ready xs_mm ln2_sums ln3_sums xmax_ready xsum_ready xsub_ready xexp_done
            xinv_ready xp_ready xp_tr xp_t_ready x2_mm x2_ready ln3_stats xn3_ready xn3_tr
            xn3_t_ready logits_mm chosen_ready counts_mm slot_ready experts_known zero_ready
            zero_out scattered routed_in0 routed_in1 routed_in2 routed_in3 routed_tr routed_t_ready
            gate_mm up_mm silu_done hidden_ready hidden_tr hidden_t_ready y_mm y_ready out_done0
            out_done1 out_done2 out_done3 units_counted beyond_found old_slots beyond_chosen
            shift_known units_placed unit_batch_known bm_ready rstd2 rstd3 vg_ready xb_ready
            gate_up_copied down_copied last_down_copied""".split()
        s = {n: sem(n) for n in names}

        block = ctx.enter_context(nc.Block())

        def bank(n):
            return ps[:, n, :]

        def logits(lo, hi):
            return bank(7 if lo < TA else 1)[:, lo * E:hi * E]

        S_BANK = (0, 1)
        ST_BANK = (2, 4)
        O_BANK = 6
        MISC = 7
        def x2_ps(t):
            return bank(5 if t % 2 else 3)[:, 0:P]

        PREP_BANK = (0, 6)

        def tile_offsets(engine, which, n, most):
            registers = [engine.alloc_register(f"offset{which}_{n}_{j}") for j in range(STRIPS)]
            engine.load(registers, unit_expert[0:1, which, STRIPS * n:STRIPS * (n + 1)])
            return [engine.snap(reg, donate=True, min_val=0, max_val=most) for reg in registers]

        @block.sync
        def _(sp):
            sp.dma_start(x_sb[:, 0:QT, :], x[0].rearrange("(t p) d -> p t d", p=P)).then_inc(s["x0_in"], 16)
            sp.dma_start(cst[:], consts).then_inc(s["const_in"], 16)
            sp.dma_start(w_attn_sb[:], w_attn).then_inc(s["w_attn_in"], 16)
            sp.dma_start(x_sb[:, QT:NT, :], x[1].rearrange("(t p) d -> p t d", p=P)).then_inc(s["x1_in"], 16)
            sp.dma_start(ctx_sb[:], ctx_t).then_inc(s["ctx_in"], 16)
            sp.dma_start(wk_sb, wk).then_inc(s["wkv_in"], 16)
            sp.dma_start(wv_sb, wv).then_inc(s["wkv_in"], 16)
            sp.dma_start(wq_sb, wq_t.rearrange("(c p) d -> p c d", p=P)).then_inc(s["wqo_in"], 16)
            sp.dma_start(wo_sb, wo.rearrange("(c p) d -> p c d", p=P)).then_inc(s["wqo_in"], 16)
            def max_rows(i):
                sp.wait_ge(s["m_t_ready"], i + 1)
                for c in range(MP):
                    sp.dma_start(qs[SC + c:SC + c + 1, GH * i:GH * (i + 1), :],
                                 m_t[GH * c:GH * (c + 1), :]).then_inc(s["m_rows_odd" if i % 2 else "m_rows_even"], 16)

            for b in range(B):
                out_sem = s[f"parts_out{b}"]
                for p, ready in enumerate(("hi_ready", "mid_ready", "low_ready")):
                    for w, dst in ((0, q_parts_dram), (1, k_parts_dram)):
                        sp.wait_ge(s[ready], 2 * b + w + 1)
                        if w == 1 and p < 2:
                            sp.dma_start(dst[b, p:p + 4:3].rearrange("c d h t -> (d h) c t"),
                                         part[:, w, p, b, :].unsqueeze(1).to_broadcast([P, 2, T])).then_inc(out_sem, 16)
                        else:
                            sp.dma_start(dst[b, p], part[:, w, p, b, :]).then_inc(out_sem, 16)
                sp.wait_ge(out_sem, 16 * 6)
                for h0, h1, in_sem in ((0, GH, s[f"stack{b}_first"]), (GH, H, s[f"stack{b}_in"])):
                    if b == 1 and h0 > 0:
                        max_rows(0)
                    for r in range(3):
                        rows, hs = slice(r * 3 * DH, (r + 1) * 3 * DH), slice(b * H + h0, b * H + h1)
                        sp.dma_start(qs[rows, hs, :],
                                     q_parts_dram[b, :, :, h0:h1].rearrange("c d h t -> (c d) h t"))\
                            .then_inc(in_sem, 16)
                        sp.dma_start(ks[rows, hs, :],
                                     k_parts_dram[b, r:r + 3, :, h0:h1].rearrange("c d h t -> (c d) h t"))\
                            .then_inc(in_sem, 16)
            sp.wait_ge(s["zero_ready"], 2)
            for i in range(NG):
                if i >= 1:
                    max_rows(i)
                if i < FILLS:
                    n = NS // FILLS
                    sp.dma_start(routed_dram[i * n * P:(i + 1) * n * P].rearrange("(s p) d -> p s d", p=P),
                                 empty_row[:, :].unsqueeze(1).to_broadcast([P, n, PW])).then_inc(s["zero_out"], 16)
            sp.wait_ge(s["st_ready"], KU * NG)
            sp.dma_start(gate_up_sb, gate_up).then_inc(s["experts_in"], 16)
            sp.dma_start(down_sb, down).then_inc(s["experts_in"], 16)
            sp.wait_ge(s["scattered"], 16 * NT)
            for c, (n0, n1) in enumerate(READS):
                sp.dma_start(routed[:, n0:n1, :],
                             routed_dram[n0 * P:n1 * P].rearrange("(s p) d -> p s d", p=P))\
                    .then_inc(s[f"routed_in{c}"], 16)

        @block.scalar
        def _(act):
            def copy(dst, src):
                return nc.scalar.activation(dst, src, ACT.Copy)

            act.dma_start(b_qk_sb[:], b_attn_qk).then_inc(s["bias_in"], 16)
            act.dma_start(b_v_sb[:], b_attn_v.partition_broadcast(P)).then_inc(s["bias_in"], 16)
            act.wait_ge(s["warm_ready"], 1)
            nc.scalar.activation(warm_act[:], warm[:, 0:1], ACT.Exp)
            def transposed(b):
                act.wait_ge(s["xn_tr"], b + 1)
                copy(xn_t[:, b, :], bank(b)).then_inc(s["xn_t_ready"], 1)

            def qk_parts(b):
                act.wait_ge(s["bias_in"], 32)
                for w in range(2):
                    n = 2 * b + w
                    act.wait_ge(s["qk_mm"], n + 1)
                    nc.scalar.activation(full[:, w, b, :], bank(2 + w), ACT.Identity,
                                         bias=b_qk_sb[:, w:w + 1]).then_inc(s["full_ready"], 1)
                    nc.scalar.activation(part[:, w, 0, b, :], bank(2 + w), ACT.Identity,
                                         bias=b_qk_sb[:, w:w + 1]).then_inc(s["hi_ready"], 1)
                for w in range(2):
                    act.wait_ge(s["rest_ready"], 2 * b + w + 1)
                    copy(part[:, w, 1, b, :], rest[:, w, b, :]).then_inc(s["mid_ready"], 1)

            def context(w, product, read, blk):
                act.wait_ge(s["kv_blk_zero"], 2)
                act.wait_ge(s[product], 1)
                for half in range(2):
                    rows = slice(64 * half, 64 * half + 64)
                    copy(blk[rows, :, :, half, :], ps[rows, 4 + w, :].rearrange("p (c b j) -> p c b j", c=XC, b=B))\
                        .then_inc(s[read], 1)

            transposed(0)
            qk_parts(0)
            act.dma_start(w_proj_sb[:], w_proj).then_inc(s["proj_in"], 16)
            act.dma_start(b_proj_sb[:], b_proj.partition_broadcast(P)).then_inc(s["xbias_in"], 16)
            act.dma_start(bo_sb[:], bo.partition_broadcast(P)).then_inc(s["xbias_in"], 16)
            act.dma_start(router_sb[:], router_t).then_inc(s["router_in"], 16)
            act.wait_ge(s["ones_ready"], 1)
            act.dma_start(ks[SC:SA, :, :], ones_row[:, :].unsqueeze(1).to_broadcast([MP, B * H, T]))\
                .then_inc(s["ones_in"], 16)
            transposed(1)
            context(0, "kt_mm", "kt_read", k_blk)
            qk_parts(1)
            context(1, "vt_mm", "vt_read", v_blk)
            for n in range(2):
                act.wait_ge(s["a_mm"], n + 1)
                copy(a_sb[:, :, n * 256:(n + 1) * 256].rearrange("p b (c j) -> p b c j", c=4),
                     ps[:, 2 + n, :].rearrange("p (c b j) -> p b c j", c=4, b=B)).then_inc(s["a_read"], 1)
            def o_copy(i):
                act.wait_ge(s["pv_done"], QT * (i + 1))
                if i >= 1:
                    act.wait_ge(s["o_tr"], i)
                copy(o_sb[:, :], bank(O_BANK)).then_inc(s["o_copied"], 1)

            def m_copy(i):
                act.wait_ge(s["m_tr"], i + 1)
                if i >= 1:
                    act.wait_ge(s["m_rows_even" if i % 2 else "m_rows_odd"], 16 * MP * ((i - 1) // 2 + 1))
                copy(m_t[:, :], bank(MISC)[0:MP * GH, 0:T // 2].bitcast(BF16)).then_inc(s["m_t_ready"], 1)

            def exps(i, kt):
                for pair in range(2):
                    u = KU * i + 2 * kt + pair
                    act.wait_ge(s["st_ready"], u + 1)
                    if i >= 1:
                        act.wait_ge(s["pv_done"], QT * (i - 1) + kt + 1)
                    bk = ST_BANK[pair]
                    nc.scalar.activation(probs[:, kt, 2 * pair:2 * pair + 2, kt * P:T],
                                         ps[:, bk:bk + 2, kt * P:T], ACT.Exp,
                                         scale=float(DH) ** -0.5).then_inc(s["exp_done"], 1)

            m_copy(0)
            act.wait_ge(s["bm_mm"], 1)
            copy(bm_sb[:].rearrange("p b c d -> p (b c d)"),
                 ps[:, 4:6, :].rearrange("p a n -> p (a n)")).then_inc(s["bm_read"], 1)
            for i in range(NG):
                exps(i, 0)
                if i >= 1:
                    o_copy(i - 1)
                if i + 1 < NG:
                    m_copy(i + 1)
                for kt in range(1, QT):
                    exps(i, kt)
            o_copy(NG - 1)

            def x2_copy(t):
                act.wait_ge(s["ln3_sums"], t + 1)
                copy(x2[:, t, :], x2_ps(t)).then_inc(s["x2_ready"], 1)

            def norm3(t):
                act.wait_ge(s["rstd3"], t + 1)
                act.wait_ge(s["x2_ready"], t + 1)
                nc.scalar.activation(xn3[:, t, :], x2[:, t, :], ACT.Identity, scale=rstd3[:, t:t + 1],
                                     bias=shift3[:, t:t + 1]).then_inc(s["xn3_ready"], 1)

            def st_d(t):
                act.wait_ge(s["xsub_ready"], t + 1)
                nc.scalar.activation(xe[:, t % 2, :], xe[:, t % 2, :], ACT.Exp,
                                     scale=float(XD) ** -0.5).then_inc(s["xexp_done"], 1)

            def st_e(t):
                act.wait_ge(s["xp_tr"], t + 1)
                if t >= 2:
                    act.wait_ge(s["x2_mm"], t - 1)
                copy(xp_t[:, t % 2, :], bank(4)).then_inc(s["xp_t_ready"], 1)

            def st_f(t):
                act.wait_ge(s["xn3_tr"], t + 1)
                if t >= 1:
                    act.wait_ge(s["logits_mm"], t)
                copy(xn3_t[:], bank(2)[:, 0:P]).then_inc(s["xn3_t_ready"], 1)

            for step in range(2, NT + 5):
                late = step >= NT + 2
                for fn, lag in ((x2_copy, 4), (st_d, 2), (st_e, 3), (norm3, 5), (st_f, 5)) if late else \
                        ((st_d, 2), (norm3, 5), (st_e, 3), (x2_copy, 4), (st_f, 5)):
                    if 0 <= step - lag < NT:
                        fn(step - lag)
                if step == 2:
                    act.wait_ge(s["attn_tr"], 2)
                    act.wait_ge(s["x1_mm"], 1)
                    copy(attn_t[:], bank(PREP_BANK[1])).then_inc(s["attn_t_ready"], 1)
                if step == QT:
                    act.wait_ge(s["xn2_tr"], 2)
                    copy(xn2_t[:, 1, :], bank(PREP_BANK[1])).then_inc(s["xn2_t_ready"], 1)

            def mx_a(n):
                act.wait_ge(s["routed_tr"], n + 1)
                if n >= 2:
                    act.wait_ge(s["up_mm"], n - 1)
                copy(routed_t[:, n % 2, :], bank(0)[:, 0:P]).then_inc(s["routed_t_ready"], 1)

            def mx_b(n):
                act.wait_ge(s["gate_mm"], n + 1)
                if n >= 2:
                    act.wait_ge(s["hidden_ready"], n - 1)
                nc.scalar.activation(act_gate[:, n % 2, :], bank(1 + n % 2)[:, 0:I], ACT.Silu)\
                    .then_inc(s["silu_done"], 1)

            def mx_c(n):
                act.wait_ge(s["hidden_tr"], n + 1)
                if n >= 2:
                    act.wait_ge(s["y_mm"], n - 1)
                copy(hidden_t[:, n % 2, 0:2, :], bank(5)[:, 0:2 * P].rearrange("p (c q) -> p c q", c=2))
                copy(hidden_t[0:IR, n % 2, 2, :], bank(5)[0:IR, 2 * P:3 * P]).then_inc(s["hidden_t_ready"], 1)

            def copy_down(n):
                if n >= 2:
                    act.wait_ge(s["y_mm"], n - 1)
                offs = tile_offsets(act, 1, n, (E - 1) * IC * D)
                for j, off in list(enumerate(offs))[1:STRIPS - 1]:
                    copy(down_unit[:, n % 2, j - 1, :], down_sb[:, bass.ds(off, IC * D)])\
                        .then_inc(s["down_copied"], 1)

            nc.scalar.activation(warm_act[:], warm[:, 0:1], ACT.Silu)
            act.wait_ge(s["experts_in"], 32)
            act.wait_ge(s["experts_known"], 2)
            copy_down(0)
            copy_down(1)
            for step in range(NS + 4):
                for fn, lag in ((mx_a, 0), (mx_b, 1), (mx_c, 2)):
                    if 0 <= step - lag < NS:
                        fn(step - lag)
                if 2 <= step - 2 < NS:
                    copy_down(step - 2)

        @block.gpsimd
        def _(pool):
            nc.gpsimd.memset(warm[:], 0.0).then_inc(s["warm_ready"], 1)
            nc.gpsimd.memset(ones_row[:], 1.0).then_inc(s["ones_ready"], 1)
            nc.gpsimd.memset(neg_half[:], -0.5).then_inc(s["pool_chain"], 1)
            nc.gpsimd.memset(empty_row[:, 0:2 * D], 0.0).then_inc(s["zero_ready"], 1)
            nc.gpsimd.memset(empty_row[:, 2 * D:PW].bitcast(I32), 2 * NT * P).then_inc(s["zero_ready"], 1)
            pool.wait_ge(s["pool_chain"], 1)
            chain = [1]

            def link(ins):
                chain[0] += 1
                ins.then_inc(s["pool_chain"], 1)
                pool.wait_ge(s["pool_chain"], chain[0])

            def inv_std(ln, b):
                pool.wait_ge(s[f"ln{ln + 1}_stats"], QT * (b + 1))
                tiles = slice(b * QT, (b + 1) * QT)
                link(nc.gpsimd.tensor_scalar(var_eps[:, ln, tiles], mv[:, ln, tiles, 1], EPS, None, ALU.add))
                nc.gpsimd.tensor_tensor(rstd[:, ln, tiles], var_eps[:, ln, tiles], neg_half[:, tiles], ALU.pow)\
                    .then_inc(s[f"rstd{ln + 1}"], 1)

            for b in range(B):
                inv_std(0, b)
            link(nc.gpsimd.memset(vg[:], 0.0))
            link(nc.gpsimd.memset(vg[:, :, :, DH:DH + 1], 1.0))
            nc.gpsimd.memset(k_blk[:], 0.0).then_inc(s["kv_blk_zero"], 1)
            nc.gpsimd.memset(v_blk[:], 0.0).then_inc(s["kv_blk_zero"], 1)
            pool.wait_ge(s["x0_in"], 16)
            pool.wait_ge(s["x1_in"], 16)
            pool.wait_ge(s["xbias_in"], 32)
            nc.gpsimd.tensor_tensor(xb[:], x_sb[:], b_proj_sb[:, :].unsqueeze(1).to_broadcast([P, NT, D]), ALU.add)\
                .then_inc(s["xb_ready"], 1)
            pool.wait_ge(s["bm_read"], 1)
            first_head = bm_sb[0:CT, :, 0, :]
            nc.gpsimd.tensor_tensor(first_head, first_head, bo_sb[0:CT, :].unsqueeze(1).to_broadcast([CT, B, D]),
                                    ALU.add).then_inc(s["bm_ready"], 1)
            pool.wait_ge(s["v_ready"], B)
            for i in range(NG):
                for kt in range(QT):
                    if i >= 1:
                        pool.wait_ge(s["pv_done"], QT * (i - 1) + kt + 1)
                    nc.gpsimd.tensor_copy(vg[:, kt, :, 0:DH],
                                          v_sb[:, QT * (i // GPB) + kt, GH * (i % GPB):GH * (i % GPB) + GH, :])\
                        .then_inc(s["vg_ready"], 1)
                    for pair in range(2):
                        pool.wait_ge(s["exp_done"], KU * i + 2 * kt + pair + 1)
                        blk = probs[:, kt, 2 * pair:2 * pair + 2, kt * P:(kt + 1) * P]
                        nc.gpsimd.affine_select(out=blk, in_=blk, compare_op=ALU.is_ge, fill=0.0, base=0,
                                                pattern=[[0, 2], [1, P]], channel_multiplier=-1)\
                            .then_inc(s["masked"], 1)
                    if (i, kt) == (NG - 2, 3):
                        inv_std(1, 0)

            def inv_std3(t):
                pool.wait_ge(s["ln3_stats"], t + 1)
                link(nc.gpsimd.tensor_scalar(var3[:, t:t + 1], mv[:, 2, t, 1:2], EPS, None, ALU.add))
                nc.gpsimd.tensor_scalar(neg_mean[:, t:t + 1], mv[:, 2, t, 0:1], -1.0, None, ALU.mult)
                link(nc.gpsimd.tensor_tensor(rstd3[:, t:t + 1], var3[:, t:t + 1], neg_half[:, 0:1], ALU.pow))
                nc.gpsimd.tensor_tensor(shift3[:, t:t + 1], neg_mean[:, t:t + 1], rstd3[:, t:t + 1], ALU.mult)\
                    .then_inc(s["rstd3"], 1)

            def probabilities(t):
                pool.wait_ge(s["xinv_ready"], t + 1)
                if t >= 2:
                    pool.wait_ge(s["xp_tr"], t - 1)
                nc.gpsimd.tensor_tensor(xp[:, t % 2, :].rearrange("p (h j) -> p h j", h=XH),
                                        xe[:, t % 2, :].rearrange("p (h j) -> p h j", h=XH),
                                        xs_sum[:, t % 2, :].unsqueeze(2).to_broadcast([P, XH, CT]), ALU.mult)\
                    .then_inc(s["xp_ready"], 1)

            for step in range(2, NT + LN3_LAG):
                if step == 3:
                    inv_std(1, 1)
                if step - 2 < NT:
                    probabilities(step - 2)
                if 0 <= step - LN3_LAG:
                    inv_std3(step - LN3_LAG)
            pool.wait_ge(s["zero_out"], 16 * FILLS)
            for t in range(NT):
                pool.wait_ge(s["xn3_ready"], t + 1)
                pool.wait_ge(s["x2_ready"], t + 1)
                pool.wait_ge(s["slot_ready"], 1 if t < TA else 2)
                nc.gpsimd.indirect_dma_start(routed_dram, bass.IndirectOffsetOnAxis(ap=slot[:, t:t + 1], axis=0),
                                             row[:, t, :], None).then_inc(s["scattered"], 16)
            for n in range(NS):
                pool.wait_ge(s["y_ready"], n + 1)
                nc.gpsimd.indirect_dma_start(
                    out.rearrange("b t d -> (b t) d"),
                    bass.IndirectOffsetOnAxis(ap=routed[:, n, 2 * D:PW].bitcast(I32), axis=0),
                    y_sb[:, n % YB, :], None, bounds_check=NT * P - 1, oob_is_err=False)\
                    .then_inc(s[f"out_done{n % YB}"], 16)
            for k in range(YB):
                pool.wait_ge(s[f"out_done{k}"], 16 * len(range(k, NS, YB)))

        @block.vector
        def _(dve):
            chain = [0]

            def link(ins):
                chain[0] += 1
                ins.then_inc(s["dve_chain"], 1)
                dve.wait_ge(s["dve_chain"], chain[0])

            v = nc.vector

            for b in range(B):
                dve.wait_ge(s[f"x{b}_in"], 16)
                for t in range(b * QT, (b + 1) * QT):
                    v.bn_stats(stat[:, 0, t, :], x_sb[:, t, :]).then_inc(s["ln1_sums"], 1)
                for t in range(b * QT, (b + 1) * QT):
                    dve.wait_ge(s["ln1_sums"], t + 1)
                    v.bn_aggr(mv[:, 0, t, :], stat[:, 0, t, :]).then_inc(s["ln1_stats"], 1)
                if b == 0:
                    v.memset(ones_bf[:], 1.0)
                    v.memset(unit_share[:], 1.0 / RR)
                    v.memset(zeros_e[:], 0.0)
                    v.memset(units_end[:, 0:1], 0.0)
                    dve.wait_ge(s["const_in"], 16)
                    v.tensor_copy(cbf[:], cst[:, 0:3 * P]).then_inc(s["const_ready"], 1)
                    v.tensor_copy(row_token, token_number)
                dve.wait_ge(s["rstd1"], b + 1)
                dve.wait_ge(s["ln1_stats"], QT * (b + 1))
                for t in range(b * QT, (b + 1) * QT):
                    v.tensor_scalar(xn[:, t, :], x_sb[:, t, :], mv[:, 0, t, 0:1], rstd[:, 0, t:t + 1], ALU.subtract,
                                    ALU.mult).then_inc(s["xn_ready"], 1)
            for b in range(B):
                for w in range(2):
                    n = 2 * b + w
                    dve.wait_ge(s["full_ready"], n + 1)
                    dve.wait_ge(s["hi_ready"], n + 1)
                    v.tensor_tensor(rest[:, w, b, :], full[:, w, b, :], part[:, w, 0, b, :], ALU.subtract)\
                        .then_inc(s["rest_ready"], 1)
                for w in range(2):
                    n = 2 * b + w
                    dve.wait_ge(s["mid_ready"], n + 1)
                    dve.wait_ge(s["rest_ready"], n + 1)
                    v.tensor_tensor(part[:, w, 2, b, :], rest[:, w, b, :], part[:, w, 1, b, :], ALU.subtract)\
                        .then_inc(s["low_ready"], 1)
                dve.wait_ge(s["v_mm"], b + 1)
                dve.wait_ge(s["bias_in"], 32)
                v.tensor_tensor(v_sb[:, b * QT:(b + 1) * QT, :, :].rearrange("p t h d -> p t (h d)"),
                                ps[:, 6 + b, :].rearrange("p (t n) -> p t n", t=QT),
                                b_v_sb[:, :].unsqueeze(1).to_broadcast([P, QT, D]), ALU.add)\
                    .then_inc(s["v_ready"], 1)

            def maxima(i, lo, hi):
                if lo == 0 and i >= 2:
                    dve.wait_ge(s["mparts_ready"], i - 1)
                for u in range(lo, hi):
                    qt, j, heads = units[u]
                    dve.wait_ge(s["unit_ready"], UNITS * i + u + 1)
                    w = (qt + 1) * P
                    v.tensor_reduce(mx[:, i % 2, qt, j:j + heads],
                                    bank(S_BANK[u % 2])[:, 0:heads * w].rearrange("p (h k) -> p h k", h=heads),
                                    AX.X, ALU.max).then_inc(s["unit_read"], 1)

            def max_parts(i):
                dve.wait_ge(s["unit_read"], UNITS * (i + 1))
                if i >= 1:
                    dve.wait_ge(s["m_tr"], i)
                hi, low = mparts[:, :, 0, :], mparts[:, :, 1, :]
                link(v.tensor_scalar(hi, mx[:, i % 2], -1.0, None, ALU.mult))
                v.scalar_tensor_tensor(out=low, in0=mx[:, i % 2], scalar=-1.0, in1=hi, op0=ALU.mult,
                                       op1=ALU.subtract).then_inc(s["mparts_ready"], 1)

            def attn_out(i):
                dve.wait_ge(s["o_tr"], i + 1)
                o = bank(MISC).rearrange("p (t h w) -> p t h w", t=QT, h=GH)
                link(v.reciprocal(den[:], o[:, :, :, DH]))
                b, g = i // GPB, i % GPB
                v.tensor_tensor(attn[:, b * QT:(b + 1) * QT, GH * g:GH * (g + 1), :], o[:, :, :, 0:DH],
                                den[:].unsqueeze(3).to_broadcast([P, QT, GH, DH]), ALU.mult)\
                    .then_inc(s["attn_ready"], 1)

            for i in range(2):
                maxima(i, 0, UNITS)
                max_parts(i)
            def x1_add(b):
                dve.wait_ge(s["x1_mm"], b + 1)
                dve.wait_ge(s["xb_ready"], 1)
                tiles = slice(b * QT, (b + 1) * QT)
                v.tensor_tensor(x1[:, tiles, :], bank(PREP_BANK[b] + 1).rearrange("p (t d) -> p t d", t=QT),
                                xb[:, tiles, :], ALU.add).then_inc(s["x1_ready"], 1)

            def ln2_sums(b):
                dve.wait_ge(s["x1_ready"], b + 1)
                for t in range(b * QT, (b + 1) * QT):
                    v.bn_stats(stat[:, 1, t, :], x1[:, t, :]).then_inc(s["ln2_sums"], 1)

            def ln2_stats(b):
                for t in range(b * QT, (b + 1) * QT):
                    dve.wait_ge(s["ln2_sums"], t + 1)
                    v.bn_aggr(mv[:, 1, t, :], stat[:, 1, t, :]).then_inc(s["ln2_stats"], 1)

            def norm2(b):
                dve.wait_ge(s["rstd2"], b + 1)
                dve.wait_ge(s["ln2_stats"], QT * (b + 1))
                if b >= 1:
                    dve.wait_ge(s["xn2_tr"], b)
                for t in range(b * QT, (b + 1) * QT):
                    v.tensor_scalar(xn2[:, t % QT, :], x1[:, t, :], mv[:, 1, t, 0:1], rstd[:, 1, t:t + 1],
                                    ALU.subtract, ALU.mult).then_inc(s["xn2_ready"], 1)

            for i in range(NG):
                if i + 2 < NG:
                    maxima(i + 2, 0, 6)
                if i == NG - 2:
                    dve.wait_ge(s["attn_tr"], 1)
                    v.tensor_copy(attn_t[:], bank(PREP_BANK[0])).then_inc(s["attn_t_ready"], 1)
                if i == NG - 1:
                    dve.wait_ge(s["xn2_tr"], 1)
                    v.tensor_copy(xn2_t[:, 0, :], bank(PREP_BANK[0])).then_inc(s["xn2_t_ready"], 1)
                if i >= 1:
                    attn_out(i - 1)
                if i + 2 < NG:
                    maxima(i + 2, 6, UNITS)
                    max_parts(i + 2)
                if i == NG - 2:
                    x1_add(0)
                    ln2_sums(0)
                    ln2_stats(0)
                    norm2(0)

            def heads(ap):
                return ap.rearrange("p (h j) -> p h j", h=XH)

            def over_keys(ap):
                return ap.unsqueeze(2).to_broadcast([P, XH, CT])

            def xmax(t):
                dve.wait_ge(s["xs_mm"], t + 1)
                v.tensor_reduce(xm[:, t % 2, :], heads(bank(t % 2)), AX.X, ALU.max).then_inc(s["xmax_ready"], 1)

            def xsub(t):
                dve.wait_ge(s["xmax_ready"], t + 1)
                if t >= 2:
                    dve.wait_ge(s["xp_ready"], t - 1)
                v.tensor_tensor(heads(xe[:, t % 2, :]), heads(bank(t % 2)), over_keys(xm[:, t % 2, :]),
                                ALU.subtract).then_inc(s["xsub_ready"], 1)

            def xsum(t):
                dve.wait_ge(s["xexp_done"], t + 1)
                v.tensor_reduce(xs_sum[:, t % 2, :], heads(xe[:, t % 2, :]), AX.X, ALU.add).then_inc(s["xsum_ready"], 1)

            def xinv(t):
                dve.wait_ge(s["xsum_ready"], t + 1)
                v.reciprocal(xs_sum[:, t % 2, :], xs_sum[:, t % 2, :]).then_inc(s["xinv_ready"], 1)

            def ln3_sums(t):
                dve.wait_ge(s["x2_mm"], t + 1)
                v.bn_stats(stat[:, 2, t, :], x2_ps(t)).then_inc(s["ln3_sums"], 1)

            def ln3_stats(t):
                dve.wait_ge(s["ln3_sums"], t + 1)
                v.bn_aggr(mv[:, 2, t, :], stat[:, 2, t, :]).then_inc(s["ln3_stats"], 1)

            xmax(0)
            xsub(0)
            attn_out(NG - 1)

            def step_work(step):
                for fn, lag in ((xsub, 2), (xmax, 1), (xsum, 2), (ln3_sums, 4), (xinv, 2), (ln3_stats, 4)):
                    if 0 <= step - lag < NT and (step, fn) != (2, xsub):
                        fn(step - lag)
                    if (step, fn) == (3, xmax):
                        x1_add(1)
                        ln2_sums(1)
                        ln2_stats(1)
                    if (step, fn) == (4, xmax):
                        norm2(1)

            def choose(batch, lo, hi):
                dve.wait_ge(s["logits_mm"], hi)
                n = hi - lo
                lg = logits(lo, hi).rearrange("p (t e) -> p t e", t=n)
                link(v.tensor_reduce(logit_max[:, lo:hi], lg, AX.X, ALU.max))
                if n <= 2:
                    for t in range(lo, hi):
                        ranked = v.scalar_tensor_tensor(out=first[:, t], in0=lg[:, t - lo], scalar=logit_max[:, t:t + 1],
                                                        in1=first_rank, op0=ALU.is_equal, op1=ALU.mult)
                    link(ranked)
                else:
                    link(v.tensor_tensor(first[:, lo:hi], lg, logit_max[:, lo:hi].unsqueeze(2).to_broadcast([P, n, E]),
                                         ALU.is_equal))
                    link(v.tensor_tensor(first[:, lo:hi], first[:, lo:hi],
                                         first_rank.unsqueeze(1).to_broadcast([P, n, E]), ALU.mult))
                link(v.tensor_reduce(first_max[:, lo:hi], first[:, lo:hi], AX.X, ALU.max))
                v.tensor_tensor(chosen_bf[:, lo:hi], first[:, lo:hi],
                                first_max[:, lo:hi].unsqueeze(2).to_broadcast([P, n, E]), ALU.is_equal)\
                    .then_inc(s["chosen_ready"], 1)

            def counted(batch, n):
                c = bank(6 + batch)
                return c[:, 0:E], c[:, E:E + n * E].rearrange("p (t e) -> p t e", t=n)

            def over_t(ap, n):
                return ap.unsqueeze(1).to_broadcast([P, n, E])

            def slots_first():
                dve.wait_ge(s["counts_mm"], 1)
                dve.wait_ge(s["chosen_ready"], 1)
                count, rank = counted(0, TA)
                link(v.tensor_scalar(units_so_far[:, 0], count, (RR - 1) / (2.0 * RR), ROUND, ALU.add, ALU.add))
                link(v.tensor_scalar(units_new[:, 0], units_so_far[:, 0], ROUND, None, ALU.subtract))
                link(v.tensor_tensor_scan(units_end[:, 1:1 + E], units_new[:, 0], zeros_e[:], 0.0, ALU.add, ALU.add))
                start = units_end[:, 0:E]
                link(v.scalar_tensor_tensor(out=slot_e[:, 0:TA], in0=over_t(start, TA), scalar=float(RR), in1=rank,
                                            op0=ALU.mult, op1=ALU.add))
                link(v.tensor_tensor(slot_e[:, 0:TA], slot_e[:, 0:TA], chosen_bf[:, 0:TA], ALU.mult))
                link(v.tensor_reduce(slot_f[:, 0:TA], slot_e[:, 0:TA], AX.X, ALU.add))
                v.tensor_copy(slot[:, 0:TA], slot_f[:, 0:TA]).then_inc(s["slot_ready"], 1)
                link(v.tensor_tensor(old_end[:], start, units_new[:, 0], ALU.add))

            def slots_second():
                n = NT - TA
                dve.wait_ge(s["counts_mm"], 2)
                dve.wait_ge(s["chosen_ready"], 2)
                count, rank = counted(1, n)
                old_start, start = units_end[:, 0:E], units_end[:, E:2 * E]
                tiles = slice(TA, NT)
                v.tensor_scalar(units_so_far[:, 1], count, (RR - 1) / (2.0 * RR), ROUND, ALU.add, ALU.add)\
                    .then_inc(s["units_counted"], 1)
                v.scalar_tensor_tensor(out=beyond[:], in0=over_t(units_new[:, 0], n), scalar=float(RR), in1=rank,
                                       op0=ALU.mult, op1=ALU.is_le).then_inc(s["beyond_found"], 1)
                dve.wait_ge(s["units_counted"], 1)
                link(v.tensor_tensor(units_new[:, 1], units_so_far[:, 1], units_so_far[:, 0], ALU.subtract))
                v.tensor_tensor_scan(units_end[:, 1 + E:1 + 2 * E], units_new[:, 1], zeros_e[:], units_end[:, E:E + 1],
                                     ALU.add, ALU.add).then_inc(s["units_placed"], 1)
                v.scalar_tensor_tensor(out=slot_e[:, tiles], in0=over_t(old_start, n), scalar=float(RR), in1=rank,
                                       op0=ALU.mult, op1=ALU.add).then_inc(s["old_slots"], 1)
                dve.wait_ge(s["beyond_found"], 1)
                v.tensor_tensor(beyond[:], beyond[:], chosen_bf[:, tiles], ALU.mult).then_inc(s["beyond_chosen"], 1)
                dve.wait_ge(s["units_placed"], 1)
                v.tensor_tensor(shift[:], start, old_end[:], ALU.subtract).then_inc(s["shift_known"], 1)
                dve.wait_ge(s["old_slots"], 1)
                link(v.tensor_tensor(slot_e[:, tiles], slot_e[:, tiles], chosen_bf[:, tiles], ALU.mult))
                dve.wait_ge(s["beyond_chosen"], 1)
                dve.wait_ge(s["shift_known"], 1)
                link(v.scalar_tensor_tensor(out=beyond[:], in0=beyond[:], scalar=float(RR), in1=over_t(shift[:], n),
                                            op0=ALU.mult, op1=ALU.mult))
                link(v.tensor_tensor(slot_e[:, tiles], slot_e[:, tiles], beyond[:], ALU.add))
                link(v.tensor_reduce(slot_f[:, tiles], slot_e[:, tiles], AX.X, ALU.add))
                v.tensor_copy(slot[:, tiles], slot_f[:, tiles]).then_inc(s["slot_ready"], 1)

            for step in range(2, NT + LN3_LAG):
                step_work(step)
                if step == TA + 5:
                    choose(0, 0, TA)
                if step == TA + 6:
                    slots_first()
            choose(1, TA, NT)
            slots_second()
            nu = NS * STRIPS
            v.tensor_tensor(in_second[:], unit_index, units_end[:, E:E + 1].to_broadcast([P, nu]), ALU.is_ge)\
                .then_inc(s["unit_batch_known"], 1)
            link(v.tensor_tensor(past[:], units_end[:, 1:1 + 2 * E].unsqueeze(1).to_broadcast([P, nu, 2 * E]),
                                 unit_index.unsqueeze(2).to_broadcast([P, nu, 2 * E]), ALU.is_le))
            link(v.tensor_reduce(ends_past[:], past[:], AX.X, ALU.add))
            dve.wait_ge(s["unit_batch_known"], 1)
            link(v.scalar_tensor_tensor(out=ends_past[:], in0=in_second[:], scalar=-float(E), in1=ends_past[:],
                                        op0=ALU.mult, op1=ALU.add))
            v.tensor_scalar(unit_expert[:, 0, :], ends_past[:], float(E - 1), float(2 * I), ALU.min, ALU.mult)\
                .then_inc(s["experts_known"], 1)
            v.tensor_scalar(unit_expert[:, 1, :], ends_past[:], float(E - 1), float(IC * D), ALU.min, ALU.mult)\
                .then_inc(s["experts_known"], 1)

            def mx_b(n):
                dve.wait_ge(s["silu_done"], n + 1)
                dve.wait_ge(s["up_mm"], n + 1)
                if n >= 2:
                    dve.wait_ge(s["hidden_tr"], n - 1)
                v.tensor_tensor(hidden[:, n % 2, :], bank(3 + n % 2)[:, 0:I], act_gate[:, n % 2, :], ALU.mult)\
                    .then_inc(s["hidden_ready"], 1)

            def mx_d(n):
                dve.wait_ge(s["y_mm"], n + 1)
                for c, (n0, _) in enumerate(READS):
                    if n == n0:
                        dve.wait_ge(s[f"routed_in{c}"], 16)
                if n >= YB:
                    dve.wait_ge(s[f"out_done{n % YB}"], 16 * (n // YB))
                v.tensor_tensor(y_sb[:, n % YB, :], bank(6 + n % 2)[:, 0:D], routed[:, n, D:2 * D], ALU.add)\
                    .then_inc(s["y_ready"], 1)

            def copy_last_down(n):
                if n >= 2:
                    dve.wait_ge(s["y_mm"], n - 1)
                j = STRIPS - 1
                off = dve.value_load(unit_expert[0:1, 1, STRIPS * n + j:STRIPS * n + j + 1],
                                     min_val=0, max_val=(E - 1) * IC * D)
                v.tensor_copy(down_unit[:, n % 2, j - 1, :], down_sb[:, bass.ds(off, IC * D)])\
                    .then_inc(s["last_down_copied"], 1)

            def copy_gate_up(n):
                if n >= 2:
                    dve.wait_ge(s["up_mm"], n - 1)
                offs = tile_offsets(dve, 0, n, (E - 1) * 2 * I)
                for j, off in list(enumerate(offs))[1:]:
                    v.tensor_copy(gate_up_unit[:, n % 2, j - 1, :], gate_up_sb[:, bass.ds(off, 2 * I)])\
                        .then_inc(s["gate_up_copied"], 1)

            dve.wait_ge(s["experts_in"], 32)
            dve.wait_ge(s["experts_known"], 2)
            for n in range(2):
                copy_gate_up(n)
                copy_last_down(n)
            for step in range(NS + 3):
                if step - 1 < NS and step >= 1:
                    mx_b(step - 1)
                if 2 <= step + 1 < NS:
                    copy_gate_up(step + 1)
                if 0 <= step - 3 < NS:
                    mx_d(step - 3)
                    if step - 1 < NS:
                        copy_last_down(step - 1)

        @block.tensor
        def _(pe):
            def mm(o, lhs, rhs, start=True, stop=True):
                return nc.tensor.matmul(o, lhs, rhs, start=start, stop=stop)

            pe.wait_ge(s["warm_ready"], 1)
            for _ in range(WARM):
                mm(bank(7), warm[:, 0:P], warm[:])
            pe.wait_ge(s["const_in"], 16)

            def transpose_input(b):
                for t in range(QT):
                    n = b * QT + t
                    pe.wait_ge(s["xn_ready"], n + 1)
                    last = nc.tensor.transpose(bank(b)[:, t * P:(t + 1) * P], xn[:, n, :], ident)
                last.then_inc(s["xn_tr"], 1)

            def qkv(b):
                pe.wait_ge(s["w_attn_in"], 16)
                pe.wait_ge(s["xn_t_ready"], b + 1)
                for w in range(2):
                    if b >= 1:
                        pe.wait_ge(s["hi_ready"], w + 1)
                    mm(bank(2 + w), w_attn_sb[:, w * D:(w + 1) * D], xn_t[:, b, :]).then_inc(s["qk_mm"], 1)
                for t in range(QT):
                    last = mm(bank(6 + b)[:, t * D:(t + 1) * D], xn_t[:, b, t * P:(t + 1) * P],
                              w_attn_sb[:, 2 * D:3 * D])
                last.then_inc(s["v_mm"], 1)

            def context(w, name, wt):
                for c in range(XC):
                    last = mm(bank(4 + w)[:, c * B * CT:(c + 1) * B * CT], wt[:, c * P:(c + 1) * P], ctx_sb[:])
                last.then_inc(s[name], 1)

            transpose_input(0)
            for _ in range(WARM_AGAIN):
                mm(bank(7), warm[:, 0:P], warm[:])
            qkv(0)
            pe.wait_ge(s["ctx_in"], 16)
            pe.wait_ge(s["wkv_in"], 32)
            context(0, "kt_mm", wk_sb)
            transpose_input(1)
            context(1, "vt_mm", wv_sb)
            qkv(1)
            def fold_a(c):
                if c == 0:
                    pe.wait_ge(s["wqo_in"], 32)
                    pe.wait_ge(s["kt_read"], 2)
                    pe.wait_ge(s["hi_ready"], 2 * B)
                last = mm(bank(2 + c // 4)[:, (c % 4) * P:(c % 4 + 1) * P], wq_sb[:, c, :],
                          k_blk[:, c].rearrange("p b h j -> p (b h j)"))
                if c % 4 == 3:
                    last.then_inc(s["a_mm"], 1)

            def fold_b(c):
                if c == 0:
                    pe.wait_ge(s["vt_read"], 2)
                rows = slice(64 * (c % 2), 64 * (c % 2) + 64)
                for b in range(B):
                    last = mm(ps[rows, 4 + b, (c // 2) * D:(c // 2 + 1) * D],
                              v_blk[:, c, b].rearrange("p h j -> p (h j)"), wo_sb[:, c, :])
                if c == XC - 1:
                    last.then_inc(s["bm_mm"], 1)

            def scores(i, lo, hi):
                for u in range(lo, hi):
                    qt, j0, heads = units[u]
                    w = (qt + 1) * P
                    n = UNITS * i + u
                    if n >= 2:
                        pe.wait_ge(s["unit_read"], n - 1)
                    for j in range(heads):
                        hh = GH * i + j0 + j
                        o = bank(S_BANK[u % 2])[:, j * w:(j + 1) * w]
                        mm(o, qs[0:SC, hh, qt * P:(qt + 1) * P], ks[0:SC, hh, 0:w], stop=False)
                        last = mm(o[:, qt * P:w], ident_bf, causal_bf, start=False)
                    last.then_inc(s["unit_ready"], 1)

            def max_transposes(i):
                pe.wait_ge(s["mparts_ready"], i + 1)
                if i >= 3:
                    pe.wait_ge(s["attn_ready"], i - 2)
                for qt in range(QT):
                    last = nc.tensor.transpose(bank(MISC)[0:MP * GH, qt * P // 2:(qt + 1) * P // 2].bitcast(BF16),
                                               mparts[:, qt].rearrange("p c h -> p (c h)"), ident_bf)
                last.then_inc(s["m_tr"], 1)

            def scores_t(i, kt, pair):
                if kt == 0 and pair == 0:
                    pe.wait_ge(s["m_rows_odd" if i % 2 else "m_rows_even"], 16 * MP * (i // 2 + 1))
                u = KU * i + 2 * kt + pair
                if u >= 2:
                    pe.wait_ge(s["exp_done"], u - 1)
                elif pair == 1:
                    pe.wait_ge(s["bm_read"], 1)
                for j in range(2):
                    hh = GH * i + 2 * pair + j
                    last = mm(bank(ST_BANK[pair] + j)[:, kt * P:T], ks[0:SA, hh, kt * P:(kt + 1) * P],
                              qs[0:SA, hh, kt * P:T])
                last.then_inc(s["st_ready"], 1)

            def weighted(i, kt):
                pe.wait_ge(s["masked"], KU * i + 2 * kt + 2)
                pe.wait_ge(s["vg_ready"], QT * i + kt + 1)
                if kt == 0 and i >= 1:
                    pe.wait_ge(s["o_copied"], i)
                for j in range(GH):
                    last = mm(ps[VW * j:VW * (j + 1), O_BANK, kt * P:T], vg[:, kt, j, :], probs[:, kt, j, kt * P:T],
                              start=(kt == 0), stop=(kt == QT - 1))
                last.then_inc(s["pv_done"], 1)

            def o_transposes(i):
                pe.wait_ge(s["o_copied"], i + 1)
                pe.wait_ge(s["m_t_ready"], min(i + 3, NG))
                if i >= 1:
                    pe.wait_ge(s["attn_ready"], i)
                for qt in range(QT):
                    last = nc.tensor.transpose(bank(MISC)[:, qt * P:(qt + 1) * P], o_sb[:, qt * P:(qt + 1) * P], ident)
                last.then_inc(s["o_tr"], 1)

            for c in range(XC):
                fold_a(c)
            pe.wait_ge(s["const_ready"], 1)
            pe.wait_ge(s["xn_t_ready"], B)
            pe.wait_ge(s["stack0_first"], 16 * 6)
            scores(0, 0, UNITS)
            pe.wait_ge(s["v_ready"], B)
            max_transposes(0)
            pe.wait_ge(s["stack0_in"], 16 * 6)
            for u in range(UNITS):
                scores(1, u, u + 1)
                for c in range(2 * u, min(2 * u + 2, XC)):
                    fold_b(c)
            pe.wait_ge(s["ones_in"], 16)
            pe.wait_ge(s["a_read"], 2)
            def attn_transposes(b):
                pe.wait_ge(s["attn_ready"], GPB * (b + 1))
                if b == 0:
                    pe.wait_ge(s["unit_read"], UNITS * NG)
                for t in range(QT):
                    last = nc.tensor.transpose(bank(PREP_BANK[b])[:, t * P:(t + 1) * P],
                                               attn[:, b * QT + t].rearrange("p h d -> p (h d)"), ident)
                last.then_inc(s["attn_tr"], 1)

            def project(b):
                pe.wait_ge(s["proj_in"], 16)
                pe.wait_ge(s["attn_t_ready"], b + 1)
                for t in range(QT):
                    last = mm(bank(PREP_BANK[b] + 1)[:, t * P:(t + 1) * P], attn_t[:, t * P:(t + 1) * P], w_proj_sb[:])
                last.then_inc(s["x1_mm"], 1)

            def xn2_transposes(b):
                for t in range(QT):
                    pe.wait_ge(s["xn2_ready"], b * QT + t + 1)
                    last = nc.tensor.transpose(bank(PREP_BANK[b])[:, t * P:(t + 1) * P], xn2[:, t, :], ident)
                last.then_inc(s["xn2_tr"], 1)

            def cross_scores(t):
                pe.wait_ge(s["xn2_t_ready"], t // QT + 1)
                if t >= 2:
                    pe.wait_ge(s["xsub_ready"], t - 1)
                mm(bank(t % 2), xn2_t[:, t // QT, (t % QT) * P:(t % QT + 1) * P], a_sb[:, t // QT, :])\
                    .then_inc(s["xs_mm"], 1)

            for i in range(NG):
                if i + 2 == GPB:
                    pe.wait_ge(s["stack1_first"], 16 * 6)
                    pe.wait_ge(s["stack1_in"], 16 * 6)
                for kt in range(QT):
                    scores_t(i, kt, 0)
                    if i + 2 < NG:
                        scores(i + 2, 3 * kt, 3 * kt + 1)
                    scores_t(i, kt, 1)
                    if i + 2 < NG:
                        scores(i + 2, 3 * kt + 1, 3 * kt + 2)
                    if kt >= 1:
                        weighted(i, kt - 1)
                    if kt == 0 and i >= 1:
                        weighted(i - 1, QT - 1)
                    if kt == 0 and i + 1 < NG:
                        max_transposes(i + 1)
                    if kt == 1 and i >= 1:
                        o_transposes(i - 1)
                    if i + 2 < NG:
                        scores(i + 2, 3 * kt + 2, 3 * kt + 3)
                    if (i, kt) == (NG - 2, 0):
                        attn_transposes(0)
                    if (i, kt) == (NG - 2, 1):
                        project(0)
                    if (i, kt) == (NG - 1, 0):
                        xn2_transposes(0)
                    if (i, kt) == (NG - 1, 2):
                        cross_scores(0)
            cross_scores(1)
            weighted(NG - 1, QT - 1)
            o_transposes(NG - 1)
            attn_transposes(1)
            pe.wait_ge(s["exp_done"], KU * NG)

            def st_e(t):
                pe.wait_ge(s["xp_ready"], t + 1)
                if t >= 1:
                    pe.wait_ge(s["xp_t_ready"], t)
                for c in range(4):
                    last = nc.tensor.transpose(bank(4)[:, c * P:(c + 1) * P], xp[:, t % 2, c * P:(c + 1) * P], ident)
                last.then_inc(s["xp_tr"], 1)

            def st_e2(t):
                pe.wait_ge(s["x1_ready"], t // QT + 1)
                if t >= 2:
                    pe.wait_ge(s["x2_ready"], t - 1)
                mm(x2_ps(t), ident, x1[:, t, :], start=True, stop=False)
                pe.wait_ge(s["xp_t_ready"], t + 1)
                if t == 0:
                    pe.wait_ge(s["bm_ready"], 1)
                for c in range(4):
                    last = mm(x2_ps(t), xp_t[:, t % 2, c * P:(c + 1) * P], bm_sb[:, t // QT, c, :],
                              start=False, stop=(c == 3))
                last.then_inc(s["x2_mm"], 1)

            def st_f(t):
                pe.wait_ge(s["xn3_ready"], t + 1)
                if t >= 1:
                    pe.wait_ge(s["xn3_t_ready"], t)
                nc.tensor.transpose(bank(2)[:, 0:P], xn3[:, t, :], ident).then_inc(s["xn3_tr"], 1)

            def st_f2(t):
                pe.wait_ge(s["xn3_t_ready"], t + 1)
                if t == 0:
                    pe.wait_ge(s["router_in"], 16)
                    pe.wait_ge(s["x1_ready"], B)
                if t == TA:
                    pe.wait_ge(s["xsub_ready"], NT)
                mm(logits(t, t + 1), xn3_t[:], router_sb[:]).then_inc(s["logits_mm"], 1)

            def counts(batch, lo, hi):
                o = bank(6 + batch)
                if batch == 0:
                    pe.wait_ge(s["xn2_t_ready"], B)
                    pe.wait_ge(s["x1_ready"], B)
                started = []

                def add(place, lhs, t, stop=False):
                    started.append(1)
                    return mm(o[:, place * E:(place + 1) * E], lhs, chosen_bf[:, t, :], start=len(started) == 1, stop=stop)

                for t in range(lo):
                    add(0, unit_share[:], t)
                    for k in range(hi - lo):
                        add(1 + k, ones_bf[:], t)
                pe.wait_ge(s["chosen_ready"], batch + 1)
                for t in range(lo, hi):
                    add(0, unit_share[:], t)
                for t in range(lo, hi):
                    for before in range(lo, t):
                        add(1 + t - lo, ones_bf[:], before)
                    last = add(1 + t - lo, before_bf, t, stop=t == hi - 1)
                last.then_inc(s["counts_mm"], 1)

            for step in range(2, NT + 5):
                late = step >= NT + 2
                for fn, lag in ((st_e, 3), (st_e2, 3), (st_f, 5), (st_f2, 5)) if late else \
                        ((st_e, 3), (cross_scores, 0), (st_f, 5), (st_e2, 3), (st_f2, 5)):
                    if 0 <= step - lag < NT and (step, fn) != (QT, cross_scores):
                        fn(step - lag)
                    if (step, fn) == (TA + 5, st_e2):
                        counts(0, 0, TA)
                    if (step, fn) == (2, cross_scores):
                        project(1)
                    if (step, fn) == (QT, st_e):
                        xn2_transposes(1)
                    if (step, fn) == (QT, st_e2):
                        cross_scores(QT)
            counts(1, TA, NT)

            pe.wait_ge(s["experts_in"], 32)
            pe.wait_ge(s["experts_known"], 2)
            first_gate_up = {}

            def find_gate_up(n):
                first_gate_up[n] = pe.value_load(unit_expert[0:1, 0, STRIPS * n:STRIPS * n + 1],
                                                 min_val=0, max_val=(E - 1) * 2 * I)

            find_gate_up(0)
            for _ in range(WARM_LATER):
                mm(bank(0), warm[:, 0:P], warm[:])

            def mx_a(n):
                for c, (n0, _) in enumerate(READS):
                    if n == n0:
                        pe.wait_ge(s[f"routed_in{c}"], 16)
                if n >= 1:
                    pe.wait_ge(s["routed_t_ready"], n)
                nc.tensor.transpose(bank(0)[:, 0:P], routed[:, n, 0:D], ident).then_inc(s["routed_tr"], 1)

            def mx_b(n):
                off = first_gate_up[n]
                pe.wait_ge(s["routed_t_ready"], n + 1)
                pe.wait_ge(s["gate_up_copied"], (STRIPS - 1) * (n + 1))
                for start, base, name, free in ((0, 1, "gate_mm", "silu_done"), (I, 3, "up_mm", "hidden_ready")):
                    if n >= 2:
                        pe.wait_ge(s[free], n - 1)
                    mm(bank(base + n % 2)[0:RR, 0:I], routed_t[:, n % 2, 0:RR], gate_up_sb[:, bass.ds(off + start, I)])
                    for j in range(1, STRIPS):
                        strip = slice(RR * j, RR * (j + 1))
                        last = mm(bank(base + n % 2)[strip, 0:I], routed_t[:, n % 2, strip],
                                  gate_up_unit[:, n % 2, j - 1, start:start + I])
                    last.then_inc(s[name], 1)

            def mx_c(n):
                pe.wait_ge(s["hidden_ready"], n + 1)
                if n >= 1:
                    pe.wait_ge(s["hidden_t_ready"], n)
                nc.tensor.transpose(bank(5)[:, 0:P], hidden[:, n % 2, 0:P], ident)
                nc.tensor.transpose(bank(5)[:, P:2 * P], hidden[:, n % 2, P:2 * P], ident)
                nc.tensor.transpose(bank(5)[0:IR, 2 * P:3 * P], hidden[:, n % 2, 2 * P:I], ident)\
                    .then_inc(s["hidden_tr"], 1)

            def mx_d(n):
                off = pe.value_load(unit_expert[0:1, 1, STRIPS * n:STRIPS * n + 1],
                                    min_val=0, max_val=(E - 1) * IC * D)
                pe.wait_ge(s["hidden_t_ready"], n + 1)
                pe.wait_ge(s["down_copied"], (STRIPS - 2) * (n + 1))
                pe.wait_ge(s["last_down_copied"], n + 1)
                if n >= 2:
                    pe.wait_ge(s["y_ready"], n - 1)
                for c, rows in enumerate((P, P, IR)):
                    ends = dict(start=(c == 0), stop=(c == IC - 1))
                    mm(bank(6 + n % 2)[0:RR, 0:D], hidden_t[0:rows, n % 2, c, 0:RR],
                       down_sb[0:rows, bass.ds(off + c * D, D)], **ends)
                    for j in range(1, STRIPS):
                        strip = slice(RR * j, RR * (j + 1))
                        last = mm(bank(6 + n % 2)[strip, 0:D], hidden_t[0:rows, n % 2, c, strip],
                                  down_unit[0:rows, n % 2, j - 1, c * D:(c + 1) * D], **ends)
                last.then_inc(s["y_mm"], 1)

            for step in range(NS + 3):
                if 1 <= step < NS:
                    find_gate_up(step)
                for fn, lag in ((mx_a, 0), (mx_b, 1), (mx_c, 2), (mx_d, 3)):
                    if 0 <= step - lag < NS:
                        fn(step - lag)


def kernel(**inputs):
    import numpy as _np
    import concourse.bacc as _bacc
    from concourse import mybir as _mybir
    from concourse.bass_utils import run_bass_kernel_spmd as _run

    a = {k: _np.asarray(v) for k, v in inputs.items()}
    consts = _np.zeros((P, CONST_W), _np.float32)
    r = _np.arange(P)
    consts[:, 0:P] = r[:, None] == r[None, :]
    consts[:, P:2 * P] = _np.where(r[None, :] <= r[:, None], 0.0, -1e30)
    consts[:, 2 * P:3 * P] = r[:, None] < r[None, :]
    o0 = 3 * P
    consts[:, o0:o0 + NS * STRIPS] = _np.arange(NS * STRIPS)
    o0 += NS * STRIPS
    consts[:, o0:o0 + E] = E - _np.arange(E)
    consts[:, CONST_W - NT:] = P * _np.arange(NT)[None, :] + r[:, None]
    down = a["L0_ffn_down_w"].transpose(0, 2, 1)
    down = _np.concatenate([down, _np.zeros((E, IC * P - I, D), down.dtype)], axis=1)
    b_attn = a["L0_attn_b_attn"]
    w_attn = a["L0_attn_W_attn"].copy()
    w_attn[:, 0:2 * D] = w_attn[:, 0:2 * D].reshape(D, 2, H, DH).transpose(0, 1, 3, 2).reshape(D, 2 * D)
    arrays = {
        "x": a["x"],
        "ctx_t": a["ctx_768"].transpose(2, 0, 1).reshape(CW, B * CT),
        "w_attn": w_attn,
        "b_attn_qk": b_attn[0:2 * D].reshape(2, H, DH).transpose(2, 1, 0).reshape(D, 2),
        "b_attn_v": b_attn[2 * D:3 * D],
        "w_proj": a["L0_attn_W_proj"],
        "b_proj": a["L0_attn_b_proj"],
        "wq_t": a["L0_xattn_Wq"].T,
        "wk": a["L0_xattn_Wk"],
        "wv": a["L0_xattn_Wv"],
        "wo": a["L0_xattn_Wo"],
        "bo": a["L0_xattn_bo"],
        "router_t": a["L0_ffn_router_w"].T,
        "gate_up": _np.stack([a["L0_ffn_gate_w"], a["L0_ffn_up_w"]], axis=1)
                      .transpose(3, 0, 1, 2).reshape(D, E * 2 * I),
        "down": down.reshape(E, IC, P, D).transpose(2, 0, 1, 3).reshape(P, E * IC * D),
        "consts": consts,
    }
    nc = _bacc.Bacc("TRN2", target_bir_lowering=False, num_devices=1)
    feed, args = {}, {}
    for name, v in arrays.items():
        v = _np.ascontiguousarray(v)
        feed[f"in_{name}"] = v
        args[name] = nc.dram_tensor(f"in_{name}", v.shape, _mybir.dt.from_np(v.dtype), kind="ExternalInput").ap()
    out = nc.dram_tensor("out_0", (B, T, D), F32, kind="ExternalOutput").ap()
    decoder_layer(nc, out=out, **args)
    got = _run(nc, [feed], core_ids=[0])
    return got.results[0]["out_0"]
```
